# Optimizing a Trainium2 kernel written in Bass

```python
import numpy as np
import jax
import jax.numpy as jnp

def _softmax(x, axis=-1):
    return jax.nn.softmax(x, axis=axis)

def _gelu(x):
    return jax.nn.gelu(x, approximate=True)

def _silu(x):
    return jax.nn.silu(x)

def _sigmoid(x):
    return jax.nn.sigmoid(x)

def _layernorm(x, axis=-1, eps=1e-05):
    m = jnp.mean(x, axis=axis, keepdims=True)
    v = jnp.var(x, axis=axis, keepdims=True)
    return (x - m) / jnp.sqrt(v + eps)

def _scatter_add(tgt, idx, src, axis=0):
    return tgt.at[idx].add(src)

def _segment_sum(src, seg, n):
    return jax.ops.segment_sum(src, seg, n)
kernel_name = 'mk_xattn_ffn_d1_seqx_r4_80b238'

def setup_inputs(seed: int=0):
    np.random.seed(seed)
    _w = jnp.asarray

    def _rec_inputs():
        import jax
        import jax.numpy as jnp
        _rk = jax.random.key(seed)
        x = -0.000125 + 0.9999 * jax.random.normal(jax.random.fold_in(_rk, 1), (4, 512, 512), jnp.float32)
        _lenS = 512 - jax.random.randint(jax.random.fold_in(_rk, 7), (4,), 0, max(1, 512 // 4) + 1, jnp.int32)
        _lenS2 = 1024 - jax.random.randint(jax.random.fold_in(_rk, 8), (4,), 0, max(1, 1024 // 4) + 1, jnp.int32)
        _ctx_2048P = jax.random.normal(jax.random.fold_in(_rk, 11), (4, 16, 512), jnp.float32)
        _ctx_2048c = jax.random.dirichlet(jax.random.fold_in(_rk, 511), 0.3 * jnp.ones((16,), jnp.float32), (4, 1024))
        _ctx_2048t = jnp.einsum('bsk,bkd->bsd', _ctx_2048c, _ctx_2048P)
        _ctx_2048t = _ctx_2048t * jax.lax.rsqrt(jnp.mean(jnp.square(_ctx_2048t)) + 1e-12) * 0.953939
        ctx_2048 = -0.000514642 + 1.00011 * (_ctx_2048t + 0.3 * jax.random.normal(jax.random.fold_in(_rk, 611), (4, 1024, 512), jnp.float32))
        _validS = jnp.arange(512)[None, :] < _lenS[:, None]
        _validS2 = jnp.arange(1024)[None, :] < _lenS2[:, None]
        _causal = jnp.tril(jnp.ones((512, 512), dtype=bool))
        mask_BxS2_bk0 = jnp.logical_not(jnp.broadcast_to(_validS2[:, :], (4, 1024)))
        return (x, ctx_2048, mask_BxS2_bk0)
    x, ctx_2048, mask_BxS2_bk0 = _rec_inputs()

    def _L0_xattn_setup():
        import jax, jax.numpy as jnp
        import numpy as np
        key = jax.random.key(seed)
        k1, k2, k3 = jax.random.split(key, 3)
        B, S, D, M = (8, 512, 512, 128)
        hidden_states = jax.random.normal(k1, (B, S, D), dtype=jnp.float32)
        memory_tokens = jax.random.normal(k2, (B, M, D), dtype=jnp.float32)
        memory_mask = jax.random.randint(k3, (B, M), 0, 2).astype(jnp.bool_)
        return {'hidden_states': hidden_states, 'memory_tokens': memory_tokens, 'memory_mask': memory_mask}
    _L0_xattn_all = _L0_xattn_setup()
    _L0_xattn_in = {k: v for k, v in _L0_xattn_all.items() if k in ()}
    del _L0_xattn_all

    def _L0_ffn_setup():
        import jax, jax.numpy as jnp
        import numpy as np
        from jax import lax
        E = 64
        TOP_K = 8
        SEL_K = 4
        THRESH = 0.5
        H = 512
        F_INT = 192
        B, S = (1, 512)
        key = jax.random.key(seed)
        k0, k1, k2, k3, k4 = jax.random.split(key, 5)
        return {'hidden_states': jax.random.normal(k0, (B, S, H), jnp.float32), 'gate_weight': jax.random.normal(k1, (E, H), jnp.float32) * 0.02, 'gate_up_proj': jax.random.normal(k2, (E, 2 * F_INT, H), jnp.float32) * 0.02, 'down_proj': jax.random.normal(k3, (E, H, F_INT), jnp.float32) * 0.02, 'similarity': jax.random.uniform(k4, (E, E), jnp.float32)}
    _L0_ffn_all = _L0_ffn_setup()
    _L0_ffn_in = {k: v for k, v in _L0_ffn_all.items() if k in ('gate_weight', 'gate_up_proj', 'down_proj', 'similarity')}
    del _L0_ffn_all
    return {'x': x, 'ctx_2048': ctx_2048, 'mask_BxS2_bk0': mask_BxS2_bk0, 'L0_ffn_gate_weight': _L0_ffn_in['gate_weight'], 'L0_ffn_gate_up_proj': _L0_ffn_in['gate_up_proj'], 'L0_ffn_down_proj': _L0_ffn_in['down_proj'], 'L0_ffn_similarity': _L0_ffn_in['similarity']}

def reference(x, ctx_2048, mask_BxS2_bk0, L0_ffn_gate_weight, L0_ffn_gate_up_proj, L0_ffn_down_proj, L0_ffn_similarity):
    import jax
    import jax.numpy as jnp

    def _L0_xattn_ref(hidden_states, memory_tokens, memory_mask):
        import jax, jax.numpy as jnp
        import numpy as np
        B, S, D = hidden_states.shape
        scale = 1.0 / jnp.sqrt(jnp.asarray(D, hidden_states.dtype))
        scores = jnp.einsum('bsd,bmd->bsm', hidden_states, memory_tokens) * scale
        neg_inf = jnp.asarray(-1e+30, scores.dtype)
        scores = jnp.where(memory_mask[:, None, :], scores, neg_inf)
        attn = jax.nn.softmax(scores, axis=-1)
        readout = jnp.einsum('bsm,bmd->bsd', attn, memory_tokens)
        valid_b = jnp.any(memory_mask, axis=-1)
        out = jnp.where(valid_b[:, None, None], readout, jnp.zeros_like(readout))
        return out

    def _L0_ffn_ref(hidden_states, gate_weight, gate_up_proj, down_proj, similarity):
        import jax, jax.numpy as jnp
        import numpy as np
        from jax import lax
        E = 64
        TOP_K = 8
        SEL_K = 4
        THRESH = 0.5
        H = 512
        F_INT = 192
        B, S = (1, 512)
        b, s, h = hidden_states.shape
        x = hidden_states.reshape(-1, h)
        logits = x @ gate_weight.T
        probs = jax.nn.softmax(logits.astype(jnp.float32), axis=-1).astype(logits.dtype)
        top_val, top_idx = lax.top_k(probs, TOP_K)
        top_val = top_val / jnp.clip(top_val.sum(-1, keepdims=True), 1e-12)
        sim = similarity.astype(jnp.float32)
        diag = jnp.arange(E)
        sim = sim.at[diag, diag].set(1.0)
        primary_mask = jnp.zeros((E,), bool).at[top_idx[:, :SEL_K].reshape(-1)].set(True)
        secondary_mask = jnp.zeros((E,), bool).at[top_idx[:, SEL_K:].reshape(-1)].set(True)
        cand = jnp.where(primary_mask[None, :], sim, -jnp.inf)
        best_primary = jnp.argmax(cand, axis=-1)
        best_sim = jnp.max(cand, axis=-1)
        replace = secondary_mask & ~primary_mask & (best_sim >= THRESH)
        mapping = jnp.where(replace, best_primary, jnp.arange(E))
        rerouted = mapping[top_idx]
        rerouted = rerouted.at[:, :SEL_K].set(top_idx[:, :SEL_K])
        flat_e = rerouted.reshape(-1)
        order = jnp.argsort(flat_e)
        tok = order // TOP_K
        xs = x[tok]
        group_sizes = jnp.zeros((E,), jnp.int32).at[flat_e].add(1)
        gu = lax.ragged_dot(xs, jnp.swapaxes(gate_up_proj, 1, 2), group_sizes)
        gate, up = jnp.split(gu, 2, axis=-1)
        hact = jax.nn.silu(gate) * up
        y = lax.ragged_dot(hact, jnp.swapaxes(down_proj, 1, 2), group_sizes)
        w = top_val.reshape(-1)[order]
        out = jnp.zeros_like(x).at[tok].add(y * w[:, None])
        return out.reshape(b, s, h)
    x = x + _L0_xattn_ref(_layernorm(x, axis=-1), ctx_2048, mask_BxS2_bk0)
    x = x + _L0_ffn_ref(_layernorm(x, axis=-1), L0_ffn_gate_weight, L0_ffn_gate_up_proj, L0_ffn_down_proj, L0_ffn_similarity)
    return x

_drawn_inputs = setup_inputs


def setup_inputs(seed=0):
    import zlib

    import numpy as np

    out = dict(_drawn_inputs(seed))
    spreads = {}
    factors = {'L0_ffn_gate_weight': 6.117, 'L0_ffn_gate_up_proj': 5.508, 'L0_ffn_down_proj': 5.494}
    for name, (base, spread) in spreads.items():
        noise = np.random.default_rng([zlib.crc32(name.encode()), seed]).standard_normal(out[name].shape)
        drawn = base * np.exp(spread * noise) if base else spread * noise
        out[name] = jnp.asarray(drawn.astype(out[name].dtype))
    for name, factor in factors.items():
        out[name] = (out[name] * factor).astype(out[name].dtype)
    return out
```

```python
from contextlib import ExitStack

import concourse.bass as bass
from concourse import mybir

F32, F32R, F16 = mybir.dt.float32, mybir.dt.float32r, mybir.dt.float16
I32, U32, U8 = mybir.dt.int32, mybir.dt.uint32, mybir.dt.uint8
ACT, ALU, AX = mybir.ActivationFunctionType, mybir.AluOpType, mybir.AxisListType
ds = bass.ds

P = 128
TOP, SEL = 8, 4
THRESH = 0.5
EPS = 1e-5
BIG = 1e30
ROUND = 12582912.0
FAR = 4096.0


def xattn_ffn(nc, x, ctx, ctxT, mask, gateT, w_in, w_out, sim, out):
    T, D = x.shape
    B, M, _ = ctx.shape
    E = gateT.shape[1]
    F2 = w_in.shape[2] // (D // P)
    F = F2 // 2
    FP = w_out.shape[1]
    NT = T // P
    TB = NT // B
    C = D // P
    MT = M // P
    FC = F // FP
    STEPS = T * TOP // P + E
    ROW = D + E
    WI, WO = C * F2, FC * D
    WE = WI + WO
    SCALE = float(D) ** -0.5
    assert STEPS % 2 == 0 and FP <= P and T <= 2048

    xt = x.rearrange("(t p) d -> t p d", p=P)
    ot = out.rearrange("(t p) d -> t p d", p=P)

    with ExitStack() as stack:
        def sb(name, shape, dt):
            return stack.enter_context(nc.sbuf_tensor(name, shape, dt))

        def ps(name, cols):
            return stack.enter_context(nc.psum_tensor(name, [P, cols], F32))

        def sem(name):
            return stack.enter_context(nc.semaphore(name))

        table = nc.dram_tensor("table", [T, ROW], F32, kind="Internal").ap()
        tt = table.rearrange("(t p) r -> t p r", p=P)

        CONSTS = 9

        x_all = sb("x_all", [P, NT, D], F32)
        raw = sb("raw", [P, 2 * C * M], F32)
        split = sb("split", [P, 4 * C * M], F32R)
        mask_u8 = sb("mask_u8", [P, B * M], U8)
        mask_bias = sb("mask_bias", [P, M], F32)
        valid = sb("valid", [P, B], F32)
        eps_c = sb("eps_c", [P, 1], F32)
        stats = sb("stats", [P, 6], F32)
        mv = sb("mv", [P, 2], F32)
        rstd = sb("rstd", [P, 1], F32)
        var_eps = sb("var_eps", [P, 1], F32)
        neg_half = sb("neg_half", [P, 1], F32)
        xq = sb("xq", [P, D], F32)
        qT_hi = sb("qT_hi", [P, C, P], F32R)
        qT_lo = sb("qT_lo", [P, C, P], F32R)
        scores = sb("scores", [P, M], F32)
        neg_max = sb("neg_max", [P, 1], F32)
        row_sum = sb("row_sum", [P, 1], F32)
        row_inv = sb("row_inv", [P, 2], F32)
        probs = sb("probs", [P, M], F32)
        pT_hi = sb("pT_hi", [P, MT, P], F32R)
        pT_lo = sb("pT_lo", [P, MT, P], F32R)
        xn = sb("xn", [P, D], F32)
        xnT = sb("xnT", [P, C, P], F32)
        gate_w = sb("gate_w", [P, C, E], F32)
        r_neg = sb("r_neg", [P, 1], F32)
        r_exp = sb("r_exp", [P, E], F32)
        r_sum = sb("r_sum", [P, 4], F32)
        r_probs = sb("r_probs", [P, E], F32)
        top_val = sb("top_val", [P, TOP], F32)
        top_idx = sb("top_idx", [P, TOP], U32)
        top_e = sb("top_e", [P, TOP], F16)
        top_w = sb("top_w", [P, TOP], F32)
        chosen = sb("chosen", [P, NT, SEL, 2, E], F16)
        weighed = sb("weighed", [P, SEL, 2, E], F32)
        w12 = sb("w12", [P, 2, E], F32)
        w12T = sb("w12T", [P, T], F32)
        c12T = sb("c12T", [P, T], F16)
        iota_e = sb("iota_e", [P, E], F16)
        ident = sb("ident", [P, P], F32)
        ident16 = sb("ident16", [P, P], F16)
        ones = sb("ones", [P, P], F32)

        b_q = ps("b_q", 512)
        b_s = ps("b_s", M)
        b_p = ps("b_p", MT * P)
        b_v = ps("b_v", 512)
        b_r = ps("b_r", 512)
        b_l = ps("b_l", 512)

        const_ready = sem("const_ready")
        ident_f16 = sem("ident_f16")
        x_loaded = sem("x_loaded")
        small_loaded = sem("small_loaded")
        k_loaded = sem("k_loaded")
        v_loaded = sem("v_loaded")
        k_hi = sem("k_hi")
        k_lo = sem("k_lo")
        v_hi = sem("v_hi")
        v_lo = sem("v_lo")
        bias_ready = sem("bias_ready")
        bias_step = sem("bias_step")
        valid_ready = sem("valid_ready")
        valid_step = sem("valid_step")
        stats_done = sem("stats_done")
        mv_done = sem("mv_done")
        half_ready = sem("half_ready")
        var_done = sem("var_done")
        rstd_done = sem("rstd_done")
        xq_ready = sem("xq_ready")
        q_transposed = sem("q_transposed")
        qT_hi_ready = sem("qT_hi_ready")
        qT_lo_ready = sem("qT_lo_ready")
        scores_done = sem("scores_done")
        biased = sem("biased")
        max_done = sem("max_done")
        neg_max_done = sem("neg_max_done")
        probs_ready = sem("probs_ready")
        p_transposed = sem("p_transposed")
        pT_hi_ready = sem("pT_hi_ready")
        pT_lo_ready = sem("pT_lo_ready")
        inv_done = sem("inv_done")
        inv_valid = sem("inv_valid")
        readout_done = sem("readout_done")
        x1_ready = sem("x1_ready")
        xn_ready = sem("xn_ready")
        x1_stored = sem("x1_stored")
        xn_stored = sem("xn_stored")
        xn_transposed = sem("xn_transposed")
        xnT_ready = sem("xnT_ready")
        logits_done = sem("logits_done")
        r_neg_done = sem("r_neg_done")
        r_exp_done = sem("r_exp_done")
        r_step = sem("r_step")
        chosen_ready = sem("chosen_ready")
        w12_ready = sem("w12_ready")
        w_step = sem("w_step")
        route_transposed = sem("route_transposed")
        c12_saved = sem("c12_saved")
        w12_saved = sem("w12_saved")

        K_HI, K_LO, V_HI, V_LO = (split[:, i * C * M:(i + 1) * C * M] for i in range(4))
        k_raw, v_raw = raw[:, :C * M], raw[:, C * M:]
        kh = K_HI.rearrange("p (c m) -> p c m", c=C)
        kl = K_LO.rearrange("p (c m) -> p c m", c=C)
        vh = V_HI.rearrange("p (j d) -> p j d", j=MT)
        vl = V_LO.rearrange("p (j d) -> p j d", j=MT)

        plan_names = ("bsel_done bsel2_done prim_done sim_done best_done besti_done map_step map_done "
                      "irT_done irT_saved cf_done uniq_done scan_done slots_done total_done bases_done "
                      "plan_done plan_saved ff_done ff_used wf_saved wf_stored look_done g_ready "
                      "flag_step hi_ready lo_ready list_done list_step idx_ready sim_loaded step_c iota_ready").split()
        S = {n: sem(n) for n in plan_names}

        def chain(eng, name, state={}):
            def step(ins):
                key = id(S[name])
                state[key] = state.get(key, 0) + 1
                ins.then_inc(S[name], 1)
                eng.wait_ge(S[name], state[key])
            return step

        simd = sb("simd", [P, E], F32)
        cand = sb("cand", [P, E], F32)
        best_v = sb("best_v", [P, 8], F32)
        best_i = sb("best_i", [P, 8], U32)
        pcol = sb("pcol", [P, 1], F32)
        p64 = sb("p64", [P, P], F32)
        pe_id = sb("pe_id", [P, 4], F32)
        reroute = sb("reroute", [P, 4], F32)
        dup = sb("dup", [P, P], F32)
        ir = sb("ir", [P, E], F32)
        ir16 = sb("ir16", [P, E], F16)
        irT = sb("irT", [E, P], F32)
        stepsE = sb("stepsE", [E, 4], F32)
        lower = sb("lower", [E, E], F32)
        iota_s = sb("iota_s", [E, 200], F32)
        cmp = sb("cmp", [E, 2, 200], F32)
        csel = sb("csel", [E, 2], F32)
        plan = sb("plan", [2, 416], I32)
        slots = sb("slots", [P, NT * TOP], F32)
        hi16 = sb("hi16", [P, NT * TOP], F16)
        lo16 = sb("lo16", [P, NT * TOP], F16)
        hi32 = sb("hi32", [P, NT * TOP], F32)
        lo32 = sb("lo32", [P, NT * TOP], F32)
        eqk = scores[:, 0:NT * TOP * TOP].rearrange("p (t k j) -> p t k j", t=NT, k=TOP)
        tri = sb("tri", [P, TOP, TOP], F32)
        seen = sb("seen", [P, NT * TOP], F32)
        tok1 = sb("tok1", [P, NT], F32)
        iota_hi = mask_bias[:].bitcast(F16)[:, 0:STEPS * TOP].rearrange("p (s k) -> p s k", k=TOP)
        iota_lo = xnT[:].rearrange("p c n -> p (c n)").bitcast(F16).rearrange("p (s k) -> p s k", k=TOP)
        lookm = weighed
        wf_sb = sb("wf_sb", [P, 2, E], F32)
        idx = sb("idx", [P, STEPS + 8], I32)
        idx_now = sb("idx_now", [P, 4], I32)
        idxf = sb("idxf", [P, STEPS + 8], F32)

        x_flat = x_all[:].rearrange("p t d -> p (t d)")
        xg = [x_flat[:, i * ROW:(i + 1) * ROW] for i in range(2)]
        xT_hi = [pT_hi[:, i * C:(i + 1) * C, :] for i in range(2)]
        xT_lo = [pT_lo[:, i * C:(i + 1) * C, :] for i in range(2)]
        act_g = x_flat[:, 2 * ROW:2 * ROW + F]
        hid = x_flat[:, 2 * ROW + F:2 * ROW + F2]
        hT_hi, hT_lo = qT_hi[:, 0:FC, :], qT_lo[:, 0:FC, :]
        y_sb = [probs[:, i * D:(i + 1) * D] for i in range(2)]

        uniq = x_all[0:E, 0:4, :].rearrange("p a b -> p (a b)")
        scan = x_all[0:E, 4:8, :].rearrange("p a b -> p (a b)")
        ones_w = x_all[0:E, 8:12, :].rearrange("p a b -> p (a b)")
        oh16 = x_all[:, 12:16, :].rearrange("p a b -> p (a b)").bitcast(F16)
        oh_hi = oh16[:, 0:STEPS * TOP].rearrange("p (s k) -> p s k", k=TOP)
        oh_lo = oh16[:, 2048:2048 + P * TOP].rearrange("p (s k) -> p s k", k=TOP)

        y_free = sem("y_free")
        idx_copied = sem("idx_copied")
        gathered = [sem("gathered0"), sem("gathered1")]
        scattered = [sem("scattered0"), sem("scattered1")]
        weights_loaded = sem("weights_loaded")
        weights_hi = sem("weights_hi")
        weights_lo = sem("weights_lo")
        x_transposed = sem("x_transposed")
        xT_hi_ready = sem("xT_hi_ready")
        xT_lo_ready = sem("xT_lo_ready")
        gate_up_done = sem("gate_up_done")
        silu_done = sem("silu_done")
        hid_ready = sem("hid_ready")
        h_transposed = sem("h_transposed")
        hT_hi_ready = sem("hT_hi_ready")
        hT_lo_ready = sem("hT_lo_ready")
        down_done = sem("down_done")
        y_ready = sem("y_ready")

        more_at = 400

        def raw_of(par):
            return raw[:, ds(par * WE, WI)], raw[0:FP, ds(par * WE + WI, WO)]

        def split_of(par, part):
            o = par * (2 * WE) + part * WE
            return split[:, ds(o, WI)], split[0:FP, ds(o + WI, WO)]

        def wait_alone(eng, semaphore, value):
            if not isinstance(value, int):
                value = eng.to_reg(value)
            eng.wait_ge(const_ready, CONSTS)
            eng.wait_ge(semaphore, value)

        block = stack.enter_context(nc.Block())

        @block.sync
        def _(sp):
            sp.dma_start(gate_w[:], gateT.rearrange("(c p) e -> p c e", p=P)).then_inc(small_loaded, 16)
            sp.dma_start(mask_u8[:], mask.rearrange("(a b) m -> a (b m)", a=1).broadcast_to([P, B * M])).then_inc(small_loaded, 16)
            sp.dma_start(simd[0:E, :], sim).then_inc(S["sim_loaded"], 16)
            sp.dma_start(simd[E:2 * E, :], sim).then_inc(S["sim_loaded"], 16)

            def load_batch(b, first):
                if not first:
                    wait_alone(sp, k_lo, b)
                    sp.wait_ge(k_loaded, b * 16)
                sp.dma_start(k_raw.rearrange("p (c m) -> p c m", c=C),
                             ctxT[ds(b, 1)].rearrange("a (c p) m -> p (a c) m", p=P)).then_inc(k_loaded, 16)
                if not first:
                    sp.wait_ge(v_lo, b)
                    sp.wait_ge(v_loaded, b * 16)
                sp.dma_start(v_raw.rearrange("p (j d) -> p j d", j=MT),
                             ctx[ds(b, 1)].rearrange("a (j p) d -> p (a j) d", p=P)).then_inc(v_loaded, 16)

            def load_x(t, first):
                if not first:
                    sp.wait_ge(x_loaded, t * 16)
                sp.dma_start(x_all[:, t, :], xt[t]).then_inc(x_loaded, 16)

            def store_tile(t, first):
                ready, stored = t + 1, t * 16
                if not isinstance(t, int):
                    ready, stored = sp.to_reg(ready), sp.to_reg(stored)
                sp.wait_ge(x1_ready, ready)
                if not first:
                    sp.wait_ge(x1_stored, stored)
                sp.dma_start(out[ds(t * P, P), :], x_all[:, t, :]).then_inc(x1_stored, 16)
                sp.wait_ge(xn_ready, t + 1)
                sp.dma_start(table[ds(t * P, P), 0:D], xn[:]).then_inc(xn_stored, 16)

            load_batch(0, True)
            load_x(0, True)
            for t in range(1, NT):
                load_x(t, False)
            load_batch(1, False)
            for t in range(TB):
                store_tile(t, t == 0)
            with sp.Fori(2, B) as b:
                load_batch(b, False)
                for j in range(TB):
                    store_tile((b - 1) * TB + j, False)
            for t in range((B - 1) * TB, NT):
                store_tile(t, False)

            def load_expert(e):
                i, o = raw_of(e % 2)
                sp.dma_start(i, w_in[ds(e, 1)].rearrange("a p n -> p (a n)")).then_inc(weights_loaded, 16)
                sp.dma_start(o, w_out[ds(e, 1)].rearrange("a p n -> p (a n)")).then_inc(weights_loaded, 16)

            sp.wait_ge(k_lo, B)
            sp.wait_ge(v_lo, B)
            load_expert(0)
            for t in range(NT):
                sp.wait_ge(S["wf_saved"], t + 1)
                if t:
                    sp.wait_ge(S["wf_stored"], 16 * t)
                sp.dma_start(tt[t][:, D:ROW], wf_sb[:, t % 2, :]).then_inc(S["wf_stored"], 16)
            sp.wait_ge(weights_loaded, 32)
            load_expert(1)
            with sp.Fori(1, E // 2) as i:
                for par in range(2):
                    e = 2 * i + par
                    wait_alone(sp, weights_lo, 4 * i + 2 * par - 2 if False else 4 * i + 2 * par - 2)
                    sp.wait_ge(weights_loaded, 32 * (2 * i + par))
                    ri, ro = raw_of(par)
                    sp.dma_start(ri, w_in[ds(e, 1)].rearrange("a p n -> p (a n)")).then_inc(weights_loaded, 16)
                    sp.dma_start(ro, w_out[ds(e, 1)].rearrange("a p n -> p (a n)")).then_inc(weights_loaded, 16)

        @block.gpsimd
        def _(pool):
            g = nc.gpsimd
            g.iota(iota_e[:], pattern=[[1, E]], base=0, channel_multiplier=0, allow_small_or_imprecise_dtypes=True).then_inc(const_ready, 1)
            g.memset(ones[:], 1.0).then_inc(const_ready, 1)
            pool.wait_ge(const_ready, 2)
            g.affine_select(out=ident[:], in_=ones[:], compare_op=ALU.is_equal, fill=0.0, base=0,
                            pattern=[[-1, P]], channel_multiplier=1).then_inc(const_ready, 1)
            g.iota(iota_s[:], pattern=[[1, 200]], base=0, channel_multiplier=0,
                   allow_small_or_imprecise_dtypes=True).then_inc(const_ready, 1)
            g.iota(tok1[:], pattern=[[P, NT]], base=1, channel_multiplier=1,
                   allow_small_or_imprecise_dtypes=True).then_inc(const_ready, 1)
            g.iota(pe_id[:, 0:1], pattern=[[0, 1]], base=0, channel_multiplier=1,
                   allow_small_or_imprecise_dtypes=True).then_inc(const_ready, 1)
            g.affine_select(out=lower[:], in_=ones[0:E, 0:E], compare_op=ALU.is_gt, fill=0.0, base=0,
                            pattern=[[1, E]], channel_multiplier=-1).then_inc(const_ready, 1)
            g.affine_select(out=tri[:], in_=ones[:, 0:TOP * TOP].rearrange("p (a b) -> p a b", a=TOP),
                            compare_op=ALU.is_gt, fill=0.0, base=0,
                            pattern=[[1, TOP], [-1, TOP]], channel_multiplier=0).then_inc(const_ready, 1)
            g.affine_select(out=csel[:], in_=ones[0:E, 0:2], compare_op=ALU.is_ge, fill=0.0, base=E - 1,
                            pattern=[[-1, 2]], channel_multiplier=-1).then_inc(const_ready, 1)

            def gather(s, par):
                g.indirect_dma_start(out=xg[par], out_offset=None, in_=table,
                                     in_offset=bass.IndirectOffsetOnAxis(ap=idx[:, s:s + 1], axis=0),
                                     bounds_check=bound, oob_is_err=False).then_inc(gathered[par], 16)

            g.memset(neg_half[:], -0.5).then_inc(half_ready, 1)
            pool.wait_ge(half_ready, 1)
            for n in range(2 * NT):
                pool.wait_ge(mv_done, n + 1)
                if n:
                    pool.wait_ge(xn_ready if n % 2 == 0 else xq_ready, (n + 1) // 2)
                g.tensor_scalar(var_eps[:], mv[:, 1:2], EPS, None, ALU.add).then_inc(var_done, 1)
                pool.wait_ge(var_done, n + 1)
                g.tensor_tensor(rstd[:], var_eps[:], neg_half[:], ALU.pow).then_inc(rstd_done, 1)

            pool.wait_ge(c12_saved, NT)
            g.iota(iota_hi, pattern=[[1, STEPS], [0, TOP]], base=0, channel_multiplier=0,
                   allow_small_or_imprecise_dtypes=True).then_inc(S["iota_ready"], 1)
            g.iota(iota_lo, pattern=[[1, P], [0, TOP]], base=0, channel_multiplier=0,
                   allow_small_or_imprecise_dtypes=True).then_inc(S["iota_ready"], 1)
            bound = pool.to_reg(T - 1)
            pool.wait_ge(S["idx_ready"], 1)
            pool.wait_ge(S["wf_stored"], 16 * NT)
            pool.wait_ge(xn_stored, 16 * NT)
            pool.wait_ge(x1_stored, 16 * NT)
            gather(0, 0)
            gather(1, 1)
            def pair(i, first):
                for par in range(2):
                    s = 2 * i + par
                    g.tensor_copy(idx_now[:, par:par + 1], idx[:, ds(s + 2, 1)]).then_inc(idx_copied, 1)
                    wait_alone(pool, idx_copied, 4 * i + 2 * par + 1)
                    wait_alone(pool, hid_ready, s + 1)
                    g.indirect_dma_start(out=xg[par], out_offset=None, in_=table,
                                         in_offset=bass.IndirectOffsetOnAxis(ap=idx_now[:, par:par + 1], axis=0),
                                         bounds_check=bound, oob_is_err=False).then_inc(gathered[par], 16)
                    if not first or par:
                        wait_alone(pool, scattered[0], 16 * i + 16 * par)
                    if not first:
                        wait_alone(pool, scattered[1], 16 * i)
                    g.sem_inc(y_free, 1)
                    g.tensor_copy(idx_now[:, 2 + par:3 + par], idx[:, ds(s, 1)]).then_inc(idx_copied, 1)
                    wait_alone(pool, idx_copied, 4 * i + 2 * par + 2)
                    wait_alone(pool, y_ready, s + 1)
                    g.indirect_dma_start(out=out, out_offset=bass.IndirectOffsetOnAxis(ap=idx_now[:, 2 + par:3 + par], axis=0),
                                         in_=y_sb[par], in_offset=None, bounds_check=bound, oob_is_err=False,
                                         compute_op=ALU.add).then_inc(scattered[par], 16)

            pool.wait_ge(S["plan_saved"], 3)
            g.sem_inc(y_free, 1)
            pair(0, True)
            more = pool.value_load(plan[0:1, more_at:more_at + 1], min_val=1, max_val=STEPS // 2 - 1)
            with pool.Fori(1, more + 1) as i:
                pair(i, False)
            for par in range(2):
                pool.wait_ge(scattered[par], 16 * more + 16)
                pool.wait_ge(gathered[par], 16 * more + 32)

        @block.scalar
        def _(act):
            a = nc.scalar

            def split_batch(b, first):
                act.wait_ge(k_loaded, 16 * (b + 1))
                if not first:
                    act.wait_ge(scores_done, TB * b)
                a.copy(K_HI, k_raw).then_inc(k_hi, 1)
                act.wait_ge(v_loaded, 16 * (b + 1))
                if not first:
                    act.wait_ge(readout_done, TB * b)
                a.copy(V_HI, v_raw).then_inc(v_hi, 1)

            def front(t, first):
                act.wait_ge(q_transposed, t + 1)
                if not first:
                    act.wait_ge(scores_done, t)
                a.copy(qT_hi[:].rearrange("p c n -> p (c n)"), b_q[:]).then_inc(qT_hi_ready, 1)

            def softmax(t, first):
                act.wait_ge(neg_max_done, t + 1)
                if not first:
                    act.wait_ge(p_transposed, t)
                a.activation(probs[:], scores[:], ACT.Exp, bias=neg_max[:, 0:1], accum_out=row_sum[:, 0:1]).then_inc(probs_ready, 1)

            def back(t, first):
                act.wait_ge(p_transposed, t + 1)
                if not first:
                    act.wait_ge(readout_done, t)
                a.copy(pT_hi[:].rearrange("p c n -> p (c n)"), b_p[:]).then_inc(pT_hi_ready, 1)

            def router(t, first):
                act.wait_ge(xn_transposed, t + 1)
                if not first:
                    act.wait_ge(logits_done, t)
                a.copy(xnT[:].rearrange("p c n -> p (c n)"), b_r[:]).then_inc(xnT_ready, 1)
                act.wait_ge(r_neg_done, t + 1)
                a.activation(r_exp[:], b_l[:, 0:E], ACT.Exp, bias=r_neg[:, 0:1], accum_out=r_sum[:, 0:1]).then_inc(r_exp_done, 1)
                act.wait_ge(probs_ready, 1)
                act.wait_ge(route_transposed, 2 * t + 2)
                a.copy(w12T[:, ds(t * P, P)], b_l[:, 256:384]).then_inc(w12_saved, 1)

            split_batch(0, True)
            for t in range(NT):
                if t % TB == 0 and t:
                    split_batch(t // TB, False)
                front(t, t == 0)
                softmax(t, t == 0)
                back(t, t == 0)
                router(t, t == 0)

            for t in range(NT):
                act.wait_ge(S["look_done"], t + 1)
                if t >= 2:
                    act.wait_ge(S["wf_stored"], 16 * (t - 1))
                a.copy(wf_sb[:, t % 2, :], (b_v, b_r)[t % 2][:, P:P + E]).then_inc(S["wf_saved"], 1)

            def split_hi(par, e1, first):
                act.wait_ge(weights_loaded, 32 * e1)
                (ri, ro), (hi_i, hi_o) = raw_of(par), split_of(par, 0)
                a.copy(hi_i, ri).then_inc(weights_hi, 1)
                a.copy(hi_o, ro).then_inc(weights_hi, 1)

            def xT(s, par):
                act.wait_ge(x_transposed, s + 1)
                a.copy(xT_hi[par].rearrange("p c n -> p (c n)"), b_q[:]).then_inc(xT_hi_ready, 1)

            def silu(s):
                act.wait_ge(gate_up_done, s + 1)
                a.activation(act_g, b_r[:, 0:F], ACT.Silu).then_inc(silu_done, 1)

            def hT(s, first):
                act.wait_ge(h_transposed, s + 1)
                a.copy(hT_hi[0:FP].rearrange("p c n -> p (c n)"), b_v[0:FP, 0:FC * P]).then_inc(hT_hi_ready, 1)

            def y(s, par):
                act.wait_ge(down_done, s + 2)
                act.wait_ge(y_free, s + 1)
                a.copy(y_sb[par], b_s[:, 0:D]).then_inc(y_ready, 1)

            def next_expert(s):
                split_it = act.value_load(plan[1:2, ds(200 + s, 1)], min_val=0, max_val=1)
                with act.If(split_it > 0):
                    e = act.value_load(plan[0:1, ds(s, 1)], min_val=0, max_val=E - 1)
                    act.wait_ge(const_ready, CONSTS)
                    act.wait_ge(down_done, s + 1)
                    act.wait_ge(weights_loaded, 32 * e + 64)
                    par = (e + 1) % 2
                    (ri, ro), (hi_i, hi_o) = raw_of(par), split_of(par, 0)
                    a.copy(hi_i, ri).then_inc(weights_hi, 1)
                    a.copy(hi_o, ro).then_inc(weights_hi, 1)

            split_hi(0, 1, True)
            xT(0, 0)
            xT(1, 1)
            silu(0)
            act.wait_ge(S["plan_saved"], 3)
            next_expert(0)
            more = act.value_load(plan[0:1, more_at:more_at + 1], min_val=1, max_val=STEPS // 2 - 1)
            with act.Fori(0, more) as i:
                for par in range(2):
                    s = 2 * i + par + 1
                    xT(s + 1, par)
                    hT(s - 1 if par else 2 * i, False)
                    silu(s)
                    y(2 * i + par, par)
                    next_expert(s)
            hT(2 * more, False)
            silu(2 * more + 1)
            y(2 * more, 0)
            hT(2 * more + 1, False)
            y(2 * more + 1, 1)

        @block.tensor
        def _(pe):
            m = nc.tensor

            def split_product(o, left, right, n):
                last = None
                for j in range(n):
                    for k, (l, r) in enumerate(((0, 0), (0, 1), (1, 0))):
                        last = m.matmul(o, left[l](j), right[r](j), start=(j == 0 and k == 0), stop=(j == n - 1 and k == 2))
                return last

            def transposes(o, src, n):
                for j in range(n):
                    last = m.transpose(o[:, j * P:(j + 1) * P], src[:, j * P:(j + 1) * P], ident[:])
                return last

            def front(t, b, first):
                pe.wait_ge(xq_ready, t + 1)
                if not first:
                    pe.wait_ge(qT_lo_ready, t)
                transposes(b_q, xq, C).then_inc(q_transposed, 1)
                pe.wait_ge(k_lo, b + 1)
                pe.wait_ge(qT_lo_ready, t + 1)
                if not first:
                    pe.wait_ge(biased, t)
                for n in range(M // 512):
                    last = split_product(b_s[:, n * 512:(n + 1) * 512],
                                         (lambda j: qT_hi[:, j, :], lambda j: qT_lo[:, j, :]),
                                         (lambda j: kh[:, j, n * 512:(n + 1) * 512], lambda j: kl[:, j, n * 512:(n + 1) * 512]), C)
                last.then_inc(scores_done, 1)

            def back(t, b, first):
                pe.wait_ge(probs_ready, t + 1)
                if not first:
                    pe.wait_ge(pT_lo_ready, t)
                transposes(b_p, probs, MT).then_inc(p_transposed, 1)
                pe.wait_ge(v_lo, b + 1)
                pe.wait_ge(pT_lo_ready, t + 1)
                if not first:
                    pe.wait_ge(x1_ready, t)
                split_product(b_v[:, 0:D], (lambda j: pT_hi[:, j, :], lambda j: pT_lo[:, j, :]),
                              (lambda j: vh[:, j, :], lambda j: vl[:, j, :]), MT).then_inc(readout_done, 1)

            def router(t, first):
                pe.wait_ge(xn_ready, t + 1)
                if not first:
                    pe.wait_ge(xnT_ready, t)
                transposes(b_r, xn, C).then_inc(xn_transposed, 1)
                pe.wait_ge(small_loaded, 32)
                pe.wait_ge(xnT_ready, t + 1)
                if not first:
                    pe.wait_ge(w12_saved, t)
                    pe.wait_ge(c12_saved, t)
                for j in range(C):
                    last = m.matmul(b_l[:, 0:E], xnT[:, j, :], gate_w[:, j, :], start=(j == 0), stop=(j == C - 1))
                last.then_inc(logits_done, 1)
                pe.wait_ge(chosen_ready, t + 1)
                pe.wait_ge(r_exp_done, t + 1)
                ch = chosen[:, t].rearrange("p k h e -> p k (h e)")
                for k in range(SEL):
                    last = m.matmul(b_l[:, P:2 * P], ch[:, k, :], ident16[:], start=(k == 0), stop=(k == SEL - 1))
                last.then_inc(route_transposed, 1)
                pe.wait_ge(w12_ready, t + 1)
                pe.wait_ge(c12_saved, t + 1)
                m.transpose(b_l[:, 256:384], w12[:].rearrange("p h e -> p (h e)"), ident[:]).then_inc(route_transposed, 1)

            pe.wait_ge(const_ready, CONSTS)
            pe.wait_ge(ident_f16, 1)
            for t in range(NT):
                front(t, t // TB, t == 0)
                back(t, t // TB, t == 0)
                router(t, t == 0)

            pe.wait_ge(w12_saved, NT)
            pe.wait_ge(S["prim_done"], 1)
            m.matmul(b_q[:, 0:E], p64[0:E, :], ident[0:E, 0:E], start=True, stop=True)
            m.matmul(b_q[:, E:E + 1], dup[0:E, :], pcol[0:E, :], start=True, stop=True).then_inc(S["bsel_done"], 1)
            pe.wait_ge(S["map_done"], 2)
            m.transpose(b_r[0:E, 0:P], ir[:], ident[:]).then_inc(S["irT_done"], 1)
            for n in range(T // 512):
                o = (b_s, b_p)[n // 2][0:E, (n % 2) * 512:(n % 2 + 1) * 512]
                m.matmul(o, ir16[:], c12T[:, n * 512:(n + 1) * 512], start=True, stop=True).then_inc(S["cf_done"], 1)
            pe.wait_ge(S["total_done"], 1)
            m.matmul(b_q[0:E, 128:129], lower[:], stepsE[:, 0:1], start=True, stop=True)
            m.matmul(b_q[0:1, 132:133], stepsE[:, 0:1], ones[0:E, 0:1], start=True, stop=True).then_inc(S["bases_done"], 1)
            pe.wait_ge(S["plan_done"], 1)
            m.matmul(b_l[0:2, 0:400], csel[:], cmp[:].rearrange("e a s -> e (a s)"), start=True, stop=True).then_inc(S["bsel2_done"], 1)
            pe.wait_ge(S["irT_saved"], 1)
            pe.wait_ge(S["slots_done"], 1)
            for t in range(NT):
                o = (b_v, b_r)[t % 2]
                if t >= 2:
                    pe.wait_ge(S["look_done"], t - 1)
                    pe.wait_ge(S["wf_saved"], t - 1)
                m.matmul(o[:, 0:P], uniq[:, t * P:(t + 1) * P], irT[:], start=True, stop=True)
                m.matmul(o[:, P:P + E], w12T[:, t * P:(t + 1) * P], ir[:], start=True, stop=True).then_inc(S["ff_done"], 1)
            pe.wait_ge(S["plan_saved"], 3)
            for t in range(NT):
                pe.wait_ge(S["lo_ready"], t + 1)
                for k in range(TOP):
                    last = m.matmul(b_l[:, 0:STEPS], oh_lo[:, :, k], oh_hi[:, :, k],
                                    start=(t == 0 and k == 0), stop=(t == NT - 1 and k == TOP - 1))
                last.then_inc(S["list_done"], 1)

            def x_transpose(s, par, nth):
                pe.wait_ge(xT_lo_ready, s) if nth else None
                pe.wait_ge(gathered[par], nth)
                transposes(b_q, xg[par], C).then_inc(x_transposed, 1)

            def gate_up(s, par):
                e = pe.value_load(plan[0:1, ds(s, 1)], min_val=0, max_val=E - 1)
                pe.wait_ge(weights_lo, 2 * e + 2)
                pe.wait_ge(xT_lo_ready, s + 1)
                wh, wl = split_of(e % 2, 0)[0], split_of(e % 2, 1)[0]
                base = (e % 2) * (2 * WE)
                split_product(b_r[:, 0:F2], (lambda j: xT_hi[par][:, j, :], lambda j: xT_lo[par][:, j, :]),
                              (lambda j: split[:, ds(base + j * F2, F2)], lambda j: split[:, ds(base + WE + j * F2, F2)]), C).then_inc(gate_up_done, 1)

            def h_transpose(s):
                pe.wait_ge(hid_ready, s + 1)
                for j in range(FC):
                    last = m.transpose(b_v[0:FP, j * P:(j + 1) * P], hid[:, j * FP:(j + 1) * FP], ident[:])
                last.then_inc(h_transposed, 1)

            def down(s):
                e = pe.value_load(plan[0:1, ds(s, 1)], min_val=0, max_val=E - 1)
                base = (e % 2) * (2 * WE) + WI
                pe.wait_ge(hT_lo_ready, s + 1)
                pe.wait_ge(y_ready, s)
                split_product(b_s[:, 0:D], (lambda j: hT_hi[0:FP, j, :], lambda j: hT_lo[0:FP, j, :]),
                              (lambda j: split[0:FP, ds(base + j * D, D)], lambda j: split[0:FP, ds(base + WE + j * D, D)]), FC).then_inc(down_done, 1)

            pe.sem_inc(down_done, 1)
            pe.wait_ge(S["idx_ready"], 1)
            pe.wait_ge(gathered[0], 16)
            transposes(b_q, xg[0], C).then_inc(x_transposed, 1)
            pe.wait_ge(gathered[1], 16)
            pe.wait_ge(xT_lo_ready, 1)
            transposes(b_q, xg[1], C).then_inc(x_transposed, 1)
            gate_up(0, 0)
            more = pe.value_load(plan[0:1, more_at:more_at + 1], min_val=1, max_val=STEPS // 2 - 1)
            h_transpose(0)
            with pe.Fori(0, more) as i:
                for par in range(2):
                    s = 2 * i + par + 1
                    pe.wait_ge(gathered[par], 16 * i + 32)
                    pe.wait_ge(xT_lo_ready, 2 * i + par + 2)
                    transposes(b_q, xg[par], C).then_inc(x_transposed, 1)
                    gate_up(s, 1 - par)
                    down(2 * i + par)
                    h_transpose(s)
            gate_up(2 * more + 1, 1)
            down(2 * more)
            h_transpose(2 * more + 1)
            down(2 * more + 1)

        @block.vector
        def _(dve):
            v = nc.vector

            def layer_norm(src, dst, n, first, ready, dst_free):
                v.bn_stats(stats[:], src).then_inc(stats_done, 1)
                dve.wait_ge(stats_done, n + 1)
                v.bn_aggr(mv[:], stats[:]).then_inc(mv_done, 1)
                dve.wait_ge(mv_done, n + 1)
                for s_, n_ in dst_free:
                    dve.wait_ge(s_, n_)
                dve.wait_ge(rstd_done, n + 1)
                v.tensor_scalar(dst, src, mv[:, 0:1], rstd[:, 0:1], ALU.subtract, ALU.mult).then_inc(ready, 1)

            def split_batch(b, first):
                dve.wait_ge(k_hi, b + 1)
                v.tensor_tensor(K_LO, k_raw, K_HI, ALU.subtract).then_inc(k_lo, 1)
                dve.wait_ge(v_hi, b + 1)
                v.tensor_tensor(V_LO, v_raw, V_HI, ALU.subtract).then_inc(v_lo, 1)
                if first:
                    dve.wait_ge(small_loaded, 32)
                else:
                    dve.wait_ge(biased, TB * b)
                v.tensor_scalar(mask_bias[:], mask_u8[:, ds(b * M, M)], BIG, -BIG, ALU.mult, ALU.add).then_inc(bias_ready, 1)

            def front(t, b, first):
                dve.wait_ge(x_loaded, 16 * (t + 1))
                layer_norm(x_all[:, t, :], xq[:], 2 * t, first, xq_ready, [] if first else [(q_transposed, t)])
                dve.wait_ge(qT_hi_ready, t + 1)
                v.tensor_tensor(qT_lo[:].rearrange("p c n -> p (c n)"), b_q[:], qT_hi[:].rearrange("p c n -> p (c n)"), ALU.subtract).then_inc(qT_lo_ready, 1)
                dve.wait_ge(scores_done, t + 1)
                dve.wait_ge(bias_ready, b + 1)
                if not first:
                    dve.wait_ge(probs_ready, t)
                v.scalar_tensor_tensor(out=scores[:], in0=b_s[:], scalar=SCALE, in1=mask_bias[:], op0=ALU.mult, op1=ALU.add).then_inc(biased, 1)
                dve.wait_ge(biased, t + 1)
                v.tensor_reduce(neg_max[:], scores[:], AX.X, ALU.max, negate=True).then_inc(neg_max_done, 1)

            def back(t, b, first):
                dve.wait_ge(probs_ready, t + 1)
                v.reciprocal(row_inv[:, 0:1], row_sum[:]).then_inc(inv_done, 1)
                dve.wait_ge(inv_done, t + 1)
                v.tensor_tensor(row_inv[:, 1:2], row_inv[:, 0:1], valid[:, ds(b, 1)], ALU.mult).then_inc(inv_valid, 1)
                dve.wait_ge(pT_hi_ready, t + 1)
                v.tensor_tensor(pT_lo[:].rearrange("p c n -> p (c n)"), b_p[:], pT_hi[:].rearrange("p c n -> p (c n)"), ALU.subtract).then_inc(pT_lo_ready, 1)
                dve.wait_ge(inv_valid, t + 1)
                dve.wait_ge(readout_done, t + 1)
                xs = x_all[:, t, :]
                v.scalar_tensor_tensor(out=xs, in0=b_v[:, 0:D], scalar=row_inv[:, 1:2], in1=xs, op0=ALU.mult, op1=ALU.add).then_inc(x1_ready, 1)
                dve.wait_ge(x1_ready, t + 1)
                layer_norm(xs, xn[:], 2 * t + 1, first, xn_ready, [] if first else [(xn_stored, 16 * t), (xn_transposed, t)])

            def router(t, first):
                dve.wait_ge(logits_done, t + 1)
                v.tensor_reduce(r_neg[:], b_l[:, 0:E], AX.X, ALU.max, negate=True).then_inc(r_neg_done, 1)
                dve.wait_ge(r_exp_done, t + 1)
                base = 8 * t
                v.reciprocal(r_sum[:, 1:2], r_sum[:, 0:1]).then_inc(r_step, 1)
                dve.wait_ge(r_step, base + 1)
                v.tensor_scalar(r_probs[:], r_exp[:], r_sum[:, 1:2], None, ALU.mult).then_inc(r_step, 1)
                dve.wait_ge(r_step, base + 2)
                v.max(top_val[:], r_probs[:]).then_inc(r_step, 1)
                dve.wait_ge(r_step, base + 3)
                v.max_index(top_idx[:], top_val[:], r_probs[:]).then_inc(r_step, 1)
                v.tensor_reduce(r_sum[:, 2:3], top_val[:], AX.X, ALU.add).then_inc(r_step, 1)
                dve.wait_ge(r_step, base + 5)
                v.tensor_copy(top_e[:], top_idx[:]).then_inc(r_step, 1)
                v.reciprocal(r_sum[:, 3:4], r_sum[:, 2:3]).then_inc(r_step, 1)
                dve.wait_ge(r_step, base + 7)
                v.tensor_scalar(top_w[:], top_val[:], r_sum[:, 3:4], None, ALU.mult).then_inc(r_step, 1)
                v.tensor_tensor(chosen[:, t], iota_e[:].unsqueeze(1).unsqueeze(1).broadcast_to([P, SEL, 2, E]),
                                top_e[:].rearrange("p (h k) -> p k h", h=2).unsqueeze(3).broadcast_to([P, SEL, 2, E]), ALU.is_equal).then_inc(chosen_ready, 1)
                dve.wait_ge(r_step, base + 8)
                dve.wait_ge(chosen_ready, t + 1)
                v.tensor_tensor(weighed[:], chosen[:, t], top_w[:].rearrange("p (h k) -> p k h", h=2).unsqueeze(3).broadcast_to([P, SEL, 2, E]), ALU.mult).then_inc(w_step, 1)
                dve.wait_ge(w_step, t + 1)
                if not first:
                    dve.wait_ge(route_transposed, 2 * t)
                v.tensor_reduce(w12[:], weighed[:].rearrange("p k h e -> p h e k"), AX.X, ALU.add).then_inc(w12_ready, 1)
                dve.wait_ge(route_transposed, 2 * t + 1)
                v.tensor_copy(c12T[:, ds(t * P, P)], b_l[:, P:2 * P]).then_inc(c12_saved, 1)

            dve.wait_ge(const_ready, CONSTS)
            v.tensor_copy(ident16[:], ident[:]).then_inc(ident_f16, 1)
            dve.wait_ge(small_loaded, 32)
            v.tensor_reduce(valid[:], mask_u8[:].rearrange("p (b m) -> p b m", b=B), AX.X, ALU.max).then_inc(valid_ready, 1)
            split_batch(0, True)
            for t in range(NT):
                if t % TB == 0 and t:
                    split_batch(t // TB, False)
                front(t, t // TB, t == 0)
                back(t, t // TB, t == 0)
                router(t, t == 0)

            step = chain(dve, "map_step")
            step(v.tensor_scalar(pe_id[:, 1:2], pe_id[:, 0:1], float(E), None, ALU.is_ge))
            step(v.scalar_tensor_tensor(out=pe_id[:, 2:3], in0=pe_id[:, 1:2], scalar=-float(E), in1=pe_id[:, 0:1], op0=ALU.mult, op1=ALU.add))
            step(v.tensor_copy(dup[0:E, 0:E], ident[0:E, 0:E]))
            step(v.tensor_copy(dup[0:E, E:P], ident[0:E, 0:E]))
            step(v.memset(ones_w, 1.0))
            dve.wait_ge(c12_saved, NT)
            step(v.tensor_reduce(reroute[:, 3:4], c12T[:], AX.X, ALU.max))
            step(v.tensor_scalar(pcol[:], reroute[:, 3:4], 0.0, None, ALU.is_gt))
            v.tensor_scalar(p64[0:E, :], ones[0:E, :], pcol[0:E, 0:1], None, ALU.mult).then_inc(S["prim_done"], 1)
            dve.wait_ge(S["sim_loaded"], 32)
            step(v.tensor_scalar(cand[:], iota_e[:], pe_id[:, 2:3], None, ALU.is_equal))
            step(v.tensor_scalar(ir[:], cand[:], -1.0, 1.0, ALU.mult, ALU.add))
            step(v.tensor_tensor(simd[:], simd[:], ir[:], ALU.mult))
            step(v.tensor_tensor(simd[:], simd[:], cand[:], ALU.add))
            dve.wait_ge(S["bsel_done"], 1)
            step(v.tensor_scalar(cand[:], b_q[:, 0:E], -1.0, 3.0e38, ALU.add, ALU.mult))
            step(v.tensor_tensor(cand[:], cand[:], simd[:], ALU.add))
            step(v.max(best_v[:], cand[:]))
            step(v.max_index(best_i[:], best_v[:], cand[:]))
            step(v.tensor_scalar(reroute[:, 0:1], best_v[:, 0:1], THRESH, None, ALU.is_ge))
            step(v.tensor_tensor(reroute[:, 0:1], reroute[:, 0:1], pcol[:], ALU.mult))
            step(v.tensor_scalar(reroute[:, 1:2], b_q[:, E:E + 1], -1.0, 1.0, ALU.mult, ALU.add))
            step(v.tensor_tensor(reroute[:, 0:1], reroute[:, 0:1], reroute[:, 1:2], ALU.mult))
            step(v.tensor_tensor(reroute[:, 0:1], reroute[:, 0:1], pe_id[:, 1:2], ALU.mult))
            step(v.tensor_copy(reroute[:, 2:3], best_i[:, 0:1]))
            step(v.tensor_tensor(reroute[:, 2:3], reroute[:, 2:3], pe_id[:, 2:3], ALU.subtract))
            step(v.scalar_tensor_tensor(out=reroute[:, 3:4], in0=reroute[:, 2:3], scalar=reroute[:, 0:1], in1=pe_id[:, 2:3], op0=ALU.mult, op1=ALU.add))
            v.tensor_scalar(ir[:], iota_e[:], reroute[:, 3:4], None, ALU.is_equal).then_inc(S["map_done"], 1)
            v.tensor_scalar(ir16[:], iota_e[:], reroute[:, 3:4], None, ALU.is_equal).then_inc(S["map_done"], 1)
            dve.wait_ge(S["irT_done"], 1)
            v.tensor_copy(irT[:], b_r[0:E, 0:P]).then_inc(S["irT_saved"], 1)
            for n in range(T // 512):
                dve.wait_ge(S["cf_done"], n + 1)
                c = slice(n * 512, (n + 1) * 512)
                v.tensor_scalar(uniq[:, c], (b_s, b_p)[n // 2][0:E, (n % 2) * 512:(n % 2 + 1) * 512], 1.0, None, ALU.min).then_inc(S["uniq_done"], 1)
                dve.wait_ge(S["uniq_done"], n + 1)
                if n:
                    dve.wait_ge(S["scan_done"], n)
                v.tensor_tensor_scan(out=scan[:, c], data0=ones_w[:, c], data1=uniq[:, c],
                                     initial=0.0 if n == 0 else scan[:, n * 512 - 1:n * 512], op0=ALU.mult, op1=ALU.add).then_inc(S["scan_done"], 1)
            dve.wait_ge(S["scan_done"], T // 512)
            step(v.tensor_scalar(stepsE[:, 1:2], scan[:, T - 1:T], 1.0 / P, 0.5 - 0.5 / P, ALU.mult, ALU.add))
            step(v.tensor_scalar(stepsE[:, 2:3], stepsE[:, 1:2], ROUND, -ROUND, ALU.add, ALU.add))
            v.tensor_scalar(stepsE[:, 0:1], stepsE[:, 2:3], 1.0, None, ALU.max).then_inc(S["total_done"], 1)
            dve.wait_ge(S["bases_done"], 1)
            step(v.tensor_copy(stepsE[:, 3:4], b_q[0:E, 128:129]))
            step(v.tensor_scalar(stepsE[:, 1:2], stepsE[:, 3:4], float(P), None, ALU.mult))
            step(v.tensor_scalar(cmp[:, 0, :], iota_s[:], stepsE[:, 3:4], None, ALU.is_ge))
            v.tensor_scalar(cmp[:, 1, :], iota_s[:], stepsE[:, 3:4], None, ALU.is_equal).then_inc(S["plan_done"], 1)
            v.scalar_tensor_tensor(out=uniq, in0=scan, scalar=stepsE[:, 1:2], in1=uniq, op0=ALU.add, op1=ALU.subtract).then_inc(S["slots_done"], 1)
            dve.wait_ge(S["bsel2_done"], 1)
            v.tensor_scalar(plan[0:1, 0:200], b_l[0:1, 0:200], -1.0, None, ALU.add).then_inc(S["plan_saved"], 1)
            v.tensor_copy(plan[:, 200:400], b_l[0:2, 200:400]).then_inc(S["plan_saved"], 1)
            step(v.tensor_scalar(reroute[0:1, 0:1], b_q[0:1, 132:133], 0.5, 0.25, ALU.mult, ALU.add))
            step(v.tensor_scalar(reroute[0:1, 1:2], reroute[0:1, 0:1], ROUND, -ROUND, ALU.add, ALU.add))
            v.tensor_scalar(plan[0:1, more_at:more_at + 1], reroute[0:1, 1:2], -1.0, None, ALU.add).then_inc(S["plan_saved"], 1)
            for t in range(NT):
                dve.wait_ge(S["ff_done"], t + 1)
                ff = (b_v, b_r)[t % 2][:, 0:P].unsqueeze(1).broadcast_to([P, SEL, P])
                v.tensor_tensor(lookm[:].rearrange("p k h e -> p k (h e)"), chosen[:, t].rearrange("p k h e -> p k (h e)"), ff, ALU.mult).then_inc(S["look_done"], 1)
                dve.wait_ge(S["look_done"], t + 1)
                v.tensor_reduce(slots[:, t * TOP:(t + 1) * TOP], lookm[:].rearrange("p k h e -> p (k h) e"), AX.X, ALU.add).then_inc(S["g_ready"], 1)
                dve.wait_ge(S["g_ready"], t + 1)
            s3 = slots[:].rearrange("p (t k) -> p t k", k=TOP)
            step(v.tensor_tensor(eqk, s3.unsqueeze(3).broadcast_to([P, NT, TOP, TOP]), s3.unsqueeze(2).broadcast_to([P, NT, TOP, TOP]), ALU.is_equal))
            step(v.tensor_tensor(eqk, eqk, tri[:].unsqueeze(1).broadcast_to([P, NT, TOP, TOP]), ALU.mult))
            step(v.tensor_reduce(seen[:], eqk.rearrange("p t k j -> p (t k) j"), AX.X, ALU.max))
            step(v.tensor_scalar(lo32[:], slots[:], 1.0 / P, -0.5 + 0.5 / P, ALU.mult, ALU.add))
            step(v.tensor_scalar(hi32[:], lo32[:], ROUND, -ROUND, ALU.add, ALU.add))
            step(v.tensor_copy(hi16[:], hi32[:]))
            step(v.scalar_tensor_tensor(out=lo32[:], in0=hi32[:], scalar=-float(P), in1=slots[:], op0=ALU.mult, op1=ALU.add))
            step(v.scalar_tensor_tensor(out=lo16[:], in0=seen[:], scalar=-2.0 * P, in1=lo32[:], op0=ALU.mult, op1=ALU.add))
            dve.wait_ge(S["iota_ready"], 2)
            for t in range(NT):
                k8 = slice(t * TOP, (t + 1) * TOP)
                if t:
                    dve.wait_ge(S["list_done"], t)
                v.tensor_tensor(oh_hi, iota_hi, hi16[:, k8].unsqueeze(1).broadcast_to([P, STEPS, TOP]), ALU.is_equal).then_inc(S["hi_ready"], 1)
                step(v.tensor_tensor(oh_lo, iota_lo, lo16[:, k8].unsqueeze(1).broadcast_to([P, P, TOP]), ALU.is_equal))
                dve.wait_ge(S["hi_ready"], t + 1)
                v.tensor_scalar(oh_lo, oh_lo, tok1[:, t:t + 1], None, ALU.mult).then_inc(S["lo_ready"], 1)
            step(v.memset(idxf[:], FAR))
            dve.wait_ge(S["list_done"], NT)
            step(v.tensor_scalar(idxf[:, 0:STEPS], b_l[:, 0:STEPS], 0.0, FAR, ALU.is_equal, ALU.mult))
            step(v.tensor_tensor(idxf[:, 0:STEPS], idxf[:, 0:STEPS], b_l[:, 0:STEPS], ALU.add))
            v.tensor_scalar(idx[:], idxf[:], -1.0, None, ALU.add).then_inc(S["idx_ready"], 1)

            def split_lo(par):
                (ri, ro), (hi_i, hi_o), (lo_i, lo_o) = raw_of(par), split_of(par, 0), split_of(par, 1)
                v.tensor_tensor(lo_i, ri, hi_i, ALU.subtract).then_inc(weights_lo, 1)
                v.tensor_tensor(lo_o, ro, hi_o, ALU.subtract).then_inc(weights_lo, 1)

            def xT(s, par):
                dve.wait_ge(xT_hi_ready, s + 1)
                v.tensor_tensor(xT_lo[par].rearrange("p c n -> p (c n)"), b_q[:], xT_hi[par].rearrange("p c n -> p (c n)"), ALU.subtract).then_inc(xT_lo_ready, 1)

            def hidden(s, par):
                e = dve.value_load(plan[0:1, ds(s, 1)], min_val=0, max_val=E - 1)
                dve.wait_ge(silu_done, s + 1)
                v.scalar_tensor_tensor(out=hid, in0=act_g, scalar=xg[par][:, ds(e + D, 1)], in1=b_r[:, F:F2], op0=ALU.mult, op1=ALU.mult).then_inc(hid_ready, 1)

            def hT(s):
                dve.wait_ge(hT_hi_ready, s + 1)
                v.tensor_tensor(hT_lo[0:FP].rearrange("p c n -> p (c n)"), b_v[0:FP, 0:FC * P], hT_hi[0:FP].rearrange("p c n -> p (c n)"), ALU.subtract).then_inc(hT_lo_ready, 1)

            def next_expert(s):
                split_it = dve.value_load(plan[1:2, ds(200 + s, 1)], min_val=0, max_val=1)
                with dve.If(split_it > 0):
                    e = dve.value_load(plan[0:1, ds(s, 1)], min_val=0, max_val=E - 1)
                    dve.wait_ge(weights_hi, 2 * e + 4)
                    split_lo((e + 1) % 2)

            dve.wait_ge(weights_hi, 2)
            split_lo(0)
            xT(0, 0)
            xT(1, 1)
            hidden(0, 0)
            next_expert(0)
            more = dve.value_load(plan[0:1, more_at:more_at + 1], min_val=1, max_val=STEPS // 2 - 1)
            with dve.Fori(0, more) as i:
                for par in range(2):
                    s = 2 * i + par + 1
                    xT(s + 1, par)
                    hT(2 * i + par)
                    hidden(s, 1 - par)
                    next_expert(s)
            hT(2 * more)
            hidden(2 * more + 1, 1)
            hT(2 * more + 1)


_INS = ["x", "ctx", "ctxT", "mask", "gateT", "w_in", "w_out", "sim"]


def kernel(x, ctx_2048, mask_BxS2_bk0, L0_ffn_gate_weight, L0_ffn_gate_up_proj, L0_ffn_down_proj, L0_ffn_similarity):
    import numpy as np
    import concourse.bacc as bacc
    from concourse.bass_utils import run_bass_kernel_spmd

    def con(a):
        return np.ascontiguousarray(a)

    x, ctx = np.asarray(x), np.asarray(ctx_2048)
    up, down = np.asarray(L0_ffn_gate_up_proj), np.asarray(L0_ffn_down_proj)
    E, F2, D = up.shape
    F = down.shape[2]
    arrays = {
        "x": con(x.reshape(-1, D)),
        "ctx": con(ctx),
        "ctxT": con(ctx.transpose(0, 2, 1)),
        "mask": con(np.asarray(mask_BxS2_bk0)),
        "gateT": con(np.asarray(L0_ffn_gate_weight).T),
        "w_in": con(up.reshape(E, F2, D // P, P).transpose(0, 3, 2, 1).reshape(E, P, -1)),
        "w_out": con(down.reshape(E, D, 2, F // 2).transpose(0, 3, 2, 1).reshape(E, F // 2, -1)),
        "sim": con(np.asarray(L0_ffn_similarity)),
    }
    nc = bacc.Bacc("TRN2", target_bir_lowering=False, num_devices=1)
    args = [nc.dram_tensor(n, arrays[n].shape, mybir.dt.from_np(arrays[n].dtype), kind="ExternalInput").ap() for n in _INS]
    out = nc.dram_tensor("out", list(arrays["x"].shape), F32, kind="ExternalOutput").ap()
    xattn_ffn(nc, *args, out)
    r = run_bass_kernel_spmd(nc, [arrays], core_ids=[0])
    return r.results[0]["out"].reshape(x.shape)
```

```python
from contextlib import ExitStack

import concourse.bass as bass
from concourse import mybir

F32, F32R, F16 = mybir.dt.float32, mybir.dt.float32r, mybir.dt.float16
I32, U32, U8 = mybir.dt.int32, mybir.dt.uint32, mybir.dt.uint8
ACT, ALU, AX = mybir.ActivationFunctionType, mybir.AluOpType, mybir.AxisListType
ds = bass.ds

P = 128
TOP, SEL = 8, 4
THRESH = 0.5
EPS = 1e-5
BIG = 1e30
ROUND = 12582912.0
FAR = 4096.0


def xattn_ffn(nc, x, ctx, ctxT, mask, gateT, w_in, w_out, sim, out):
    T, D = x.shape
    B, M, _ = ctx.shape
    E = gateT.shape[1]
    F2 = w_in.shape[2] // (D // P)
    F = F2 // 2
    FP = w_out.shape[1]
    NT = T // P
    TB = NT // B
    C = D // P
    MT = M // P
    FC = F // FP
    STEPS = T * TOP // P + E
    ROW = D + E
    WI, WO = C * F2, FC * D
    WE = WI + WO
    SCALE = float(D) ** -0.5
    assert STEPS % 2 == 0 and FP <= P and T <= 2048

    xt = x.rearrange("(t p) d -> t p d", p=P)
    ot = out.rearrange("(t p) d -> t p d", p=P)

    with ExitStack() as stack:
        def sb(name, shape, dt):
            return stack.enter_context(nc.sbuf_tensor(name, shape, dt))

        def ps(name, cols):
            return stack.enter_context(nc.psum_tensor(name, [P, cols], F32))

        def sem(name):
            return stack.enter_context(nc.semaphore(name))

        table = nc.dram_tensor("table", [T, ROW], F32, kind="Internal").ap()
        tt = table.rearrange("(t p) r -> t p r", p=P)

        CONSTS = 9

        x_all = sb("x_all", [P, NT, D], F32)
        raw = sb("raw", [P, 2 * C * M], F32)
        split = sb("split", [P, 4 * C * M], F32R)
        mask_u8 = sb("mask_u8", [P, B * M], U8)
        mask_bias = sb("mask_bias", [P, M], F32)
        valid = sb("valid", [P, B], F32)
        eps_c = sb("eps_c", [P, 1], F32)
        stats = sb("stats", [P, 6], F32)
        mv = sb("mv", [P, 2], F32)
        rstd = sb("rstd", [P, 1], F32)
        var_eps = sb("var_eps", [P, 1], F32)
        neg_half = sb("neg_half", [P, 1], F32)
        xq = sb("xq", [P, D], F32)
        qT_hi = sb("qT_hi", [P, C, P], F32R)
        qT_lo = sb("qT_lo", [P, C, P], F32R)
        scores = sb("scores", [P, M], F32)
        neg_max = sb("neg_max", [P, 1], F32)
        row_sum = sb("row_sum", [P, 1], F32)
        row_inv = sb("row_inv", [P, 2], F32)
        probs = sb("probs", [P, M], F32)
        pT_hi = sb("pT_hi", [P, MT, P], F32R)
        pT_lo = sb("pT_lo", [P, MT, P], F32R)
        xn = sb("xn", [P, D], F32)
        xnT = sb("xnT", [P, C, P], F32)
        gate_w = sb("gate_w", [P, C, E], F32)
        r_neg = sb("r_neg", [P, 1], F32)
        r_exp = sb("r_exp", [P, E], F32)
        r_sum = sb("r_sum", [P, 4], F32)
        r_probs = sb("r_probs", [P, E], F32)
        top_val = sb("top_val", [P, TOP], F32)
        top_idx = sb("top_idx", [P, TOP], U32)
        top_e = sb("top_e", [P, TOP], F16)
        top_w = sb("top_w", [P, TOP], F32)
        chosen = sb("chosen", [P, NT, SEL, 2, E], F16)
        weighed = sb("weighed", [P, SEL, 2, E], F32)
        w12 = sb("w12", [P, 2, E], F32)
        w12T = sb("w12T", [P, T], F32)
        c12T = sb("c12T", [P, T], F16)
        iota_e = sb("iota_e", [P, E], F16)
        ident = sb("ident", [P, P], F32)
        ident16 = sb("ident16", [P, P], F16)
        ones = sb("ones", [P, P], F32)

        b_q = ps("b_q", 512)
        b_s = ps("b_s", M)
        b_p = ps("b_p", MT * P)
        b_v = ps("b_v", 512)
        b_r = ps("b_r", 512)
        b_l = ps("b_l", 512)

        const_ready = sem("const_ready")
        ident_f16 = sem("ident_f16")
        x_loaded = sem("x_loaded")
        small_loaded = sem("small_loaded")
        k_loaded = sem("k_loaded")
        v_loaded = sem("v_loaded")
        k_hi = sem("k_hi")
        k_lo = sem("k_lo")
        v_hi = sem("v_hi")
        v_lo = sem("v_lo")
        bias_ready = sem("bias_ready")
        bias_step = sem("bias_step")
        valid_ready = sem("valid_ready")
        valid_step = sem("valid_step")
        stats_done = sem("stats_done")
        mv_done = sem("mv_done")
        half_ready = sem("half_ready")
        var_done = sem("var_done")
        rstd_done = sem("rstd_done")
        xq_ready = sem("xq_ready")
        q_transposed = sem("q_transposed")
        qT_hi_ready = sem("qT_hi_ready")
        qT_lo_ready = sem("qT_lo_ready")
        scores_done = sem("scores_done")
        biased = sem("biased")
        max_done = sem("max_done")
        neg_max_done = sem("neg_max_done")
        probs_ready = sem("probs_ready")
        p_transposed = sem("p_transposed")
        pT_hi_ready = sem("pT_hi_ready")
        pT_lo_ready = sem("pT_lo_ready")
        inv_done = sem("inv_done")
        inv_valid = sem("inv_valid")
        readout_done = sem("readout_done")
        x1_ready = sem("x1_ready")
        xn_ready = sem("xn_ready")
        x1_stored = sem("x1_stored")
        xn_stored = sem("xn_stored")
        xn_transposed = sem("xn_transposed")
        xnT_ready = sem("xnT_ready")
        logits_done = sem("logits_done")
        r_neg_done = sem("r_neg_done")
        r_exp_done = sem("r_exp_done")
        r_step = sem("r_step")
        chosen_ready = sem("chosen_ready")
        w12_ready = sem("w12_ready")
        w_step = sem("w_step")
        route_transposed = sem("route_transposed")
        c12_saved = sem("c12_saved")
        w12_saved = sem("w12_saved")

        K_HI, K_LO, V_HI, V_LO = (split[:, i * C * M:(i + 1) * C * M] for i in range(4))
        k_raw, v_raw = raw[:, :C * M], raw[:, C * M:]
        kh = K_HI.rearrange("p (c m) -> p c m", c=C)
        kl = K_LO.rearrange("p (c m) -> p c m", c=C)
        vh = V_HI.rearrange("p (j d) -> p j d", j=MT)
        vl = V_LO.rearrange("p (j d) -> p j d", j=MT)

        plan_names = ("bsel_done bsel2_done prim_done sim_done best_done besti_done map_step map_done "
                      "irT_done irT_saved cf_done uniq_done scan_done slots_done total_done bases_done "
                      "plan_done plan_saved ff_done ff_used wf_saved wf_stored look_done g_ready "
                      "flag_step hi_ready lo_ready list_done list_step idx_ready sim_loaded step_c iota_ready").split()
        S = {n: sem(n) for n in plan_names}

        def chain(eng, name, state={}):
            def step(ins):
                key = id(S[name])
                state[key] = state.get(key, 0) + 1
                ins.then_inc(S[name], 1)
                eng.wait_ge(S[name], state[key])
            return step

        simd = sb("simd", [P, E], F32)
        cand = sb("cand", [P, E], F32)
        best_v = sb("best_v", [P, 8], F32)
        best_i = sb("best_i", [P, 8], U32)
        pcol = sb("pcol", [P, 1], F32)
        p64 = sb("p64", [P, P], F32)
        pe_id = sb("pe_id", [P, 4], F32)
        reroute = sb("reroute", [P, 4], F32)
        dup = sb("dup", [P, P], F32)
        ir = sb("ir", [P, E], F32)
        ir16 = sb("ir16", [P, E], F16)
        irT = sb("irT", [E, P], F32)
        stepsE = sb("stepsE", [E, 4], F32)
        lower = sb("lower", [E, E], F32)
        iota_s = sb("iota_s", [E, 200], F32)
        cmp = sb("cmp", [E, 2, 200], F32)
        csel = sb("csel", [E, 2], F32)
        plan = sb("plan", [2, 416], I32)
        slots = sb("slots", [P, NT * TOP], F32)
        hi16 = sb("hi16", [P, NT * TOP], F16)
        lo16 = sb("lo16", [P, NT * TOP], F16)
        hi32 = sb("hi32", [P, NT * TOP], F32)
        lo32 = sb("lo32", [P, NT * TOP], F32)
        eqk = scores[:, 0:NT * TOP * TOP].rearrange("p (t k j) -> p t k j", t=NT, k=TOP)
        tri = sb("tri", [P, TOP, TOP], F32)
        seen = sb("seen", [P, NT * TOP], F32)
        tok1 = sb("tok1", [P, NT], F32)
        iota_hi = mask_bias[:].bitcast(F16)[:, 0:STEPS * TOP].rearrange("p (s k) -> p s k", k=TOP)
        iota_lo = xnT[:].rearrange("p c n -> p (c n)").bitcast(F16).rearrange("p (s k) -> p s k", k=TOP)
        lookm = weighed
        wf_sb = sb("wf_sb", [P, 2, E], F32)
        idx = sb("idx", [P, STEPS + 8], I32)
        idx_now = sb("idx_now", [P, 4], I32)
        idxf = sb("idxf", [P, STEPS + 8], F32)

        x_flat = x_all[:].rearrange("p t d -> p (t d)")
        xg = [x_flat[:, i * ROW:(i + 1) * ROW] for i in range(2)]
        xT_hi = [pT_hi[:, i * C:(i + 1) * C, :] for i in range(2)]
        xT_lo = [pT_lo[:, i * C:(i + 1) * C, :] for i in range(2)]
        w_row = [x_flat[:, 2 * ROW + F2 + i * E:2 * ROW + F2 + (i + 1) * E] for i in range(2)]
        act_g = x_flat[:, 2 * ROW:2 * ROW + F]
        hid = x_flat[:, 2 * ROW + F:2 * ROW + F2]
        hT_hi, hT_lo = qT_hi[:, 0:FC, :], qT_lo[:, 0:FC, :]
        y_sb = [probs[:, i * D:(i + 1) * D] for i in range(2)]

        uniq = x_all[0:E, 0:4, :].rearrange("p a b -> p (a b)")
        scan = x_all[0:E, 4:8, :].rearrange("p a b -> p (a b)")
        ones_w = x_all[0:E, 8:12, :].rearrange("p a b -> p (a b)")
        oh16 = x_all[:, 12:16, :].rearrange("p a b -> p (a b)").bitcast(F16)
        oh_hi = oh16[:, 0:STEPS * TOP].rearrange("p (s k) -> p s k", k=TOP)
        oh_lo = oh16[:, 2048:2048 + P * TOP].rearrange("p (s k) -> p s k", k=TOP)

        w_kept = sem("w_kept")
        idx_copied = sem("idx_copied")
        gathered = [sem("gathered0"), sem("gathered1")]
        scattered = [sem("scattered0"), sem("scattered1")]
        weights_loaded = sem("weights_loaded")
        weights_hi = sem("weights_hi")
        weights_lo = sem("weights_lo")
        x_transposed = sem("x_transposed")
        xT_hi_ready = sem("xT_hi_ready")
        xT_lo_ready = sem("xT_lo_ready")
        gate_up_done = sem("gate_up_done")
        silu_done = sem("silu_done")
        hid_ready = sem("hid_ready")
        h_transposed = sem("h_transposed")
        hT_hi_ready = sem("hT_hi_ready")
        hT_lo_ready = sem("hT_lo_ready")
        down_done = sem("down_done")
        y_ready = sem("y_ready")

        more_at = 400

        def raw_of(par):
            return raw[:, ds(par * WE, WI)], raw[0:FP, ds(par * WE + WI, WO)]

        def pieces(buf, part):
            o = buf * (2 * WE) + part * WE
            return (split[:, ds(o, WI // 2)], split[:, ds(o + WI // 2, WI // 2)], split[0:FP, ds(o + WI, WO)])

        def raw_pieces(par):
            o = par * WE
            return (raw[:, ds(o, WI // 2)], raw[:, ds(o + WI // 2, WI // 2)], raw[0:FP, ds(o + WI, WO)])

        def wait_alone(eng, semaphore, value):
            if not isinstance(value, int):
                value = eng.to_reg(value)
            eng.wait_ge(const_ready, CONSTS)
            eng.wait_ge(semaphore, value)

        block = stack.enter_context(nc.Block())

        @block.sync
        def _(sp):
            sp.dma_start(gate_w[:], gateT.rearrange("(c p) e -> p c e", p=P)).then_inc(small_loaded, 16)
            sp.dma_start(mask_u8[:], mask.rearrange("(a b) m -> a (b m)", a=1).broadcast_to([P, B * M])).then_inc(small_loaded, 16)
            sp.dma_start(simd[0:E, :], sim).then_inc(S["sim_loaded"], 16)
            sp.dma_start(simd[E:2 * E, :], sim).then_inc(S["sim_loaded"], 16)

            def load_batch(b, first):
                if not first:
                    wait_alone(sp, k_lo, b)
                    sp.wait_ge(k_loaded, b * 16)
                sp.dma_start(k_raw.rearrange("p (c m) -> p c m", c=C),
                             ctxT[ds(b, 1)].rearrange("a (c p) m -> p (a c) m", p=P)).then_inc(k_loaded, 16)
                if not first:
                    sp.wait_ge(v_lo, b)
                    sp.wait_ge(v_loaded, b * 16)
                sp.dma_start(v_raw.rearrange("p (j d) -> p j d", j=MT),
                             ctx[ds(b, 1)].rearrange("a (j p) d -> p (a j) d", p=P)).then_inc(v_loaded, 16)

            def load_x(t, first):
                if not first:
                    sp.wait_ge(x_loaded, t * 16)
                sp.dma_start(x_all[:, t, :], xt[t]).then_inc(x_loaded, 16)

            def store_tile(t, first):
                ready, stored = t + 1, t * 16
                if not isinstance(t, int):
                    ready, stored = sp.to_reg(ready), sp.to_reg(stored)
                sp.wait_ge(x1_ready, ready)
                if not first:
                    sp.wait_ge(x1_stored, stored)
                sp.dma_start(out[ds(t * P, P), :], x_all[:, t, :]).then_inc(x1_stored, 16)
                sp.wait_ge(xn_ready, t + 1)
                sp.dma_start(table[ds(t * P, P), 0:D], xn[:]).then_inc(xn_stored, 16)

            load_batch(0, True)
            load_x(0, True)
            for t in range(1, NT):
                load_x(t, False)
            load_batch(1, False)
            for t in range(TB):
                store_tile(t, t == 0)
            with sp.Fori(2, B) as b:
                load_batch(b, False)
                for j in range(TB):
                    store_tile((b - 1) * TB + j, False)
            for t in range((B - 1) * TB, NT):
                store_tile(t, False)

            def load_expert(e):
                i, o = raw_of(e % 2)
                sp.dma_start(i, w_in[ds(e, 1)].rearrange("a p n -> p (a n)")).then_inc(weights_loaded, 16)
                sp.dma_start(o, w_out[ds(e, 1)].rearrange("a p n -> p (a n)")).then_inc(weights_loaded, 16)

            sp.wait_ge(k_lo, B)
            sp.wait_ge(v_lo, B)
            load_expert(0)
            for t in range(NT):
                sp.wait_ge(S["wf_saved"], t + 1)
                if t:
                    sp.wait_ge(S["wf_stored"], 16 * t)
                sp.dma_start(tt[t][:, D:ROW], wf_sb[:, t % 2, :]).then_inc(S["wf_stored"], 16)
            sp.wait_ge(weights_loaded, 32)
            load_expert(1)
            with sp.Fori(1, E // 2) as i:
                for par in range(2):
                    e = 2 * i + par
                    wait_alone(sp, weights_lo, 6 * i + 3 * par - 3)
                    sp.wait_ge(weights_loaded, 32 * (2 * i + par))
                    ri, ro = raw_of(par)
                    sp.dma_start(ri, w_in[ds(e, 1)].rearrange("a p n -> p (a n)")).then_inc(weights_loaded, 16)
                    sp.dma_start(ro, w_out[ds(e, 1)].rearrange("a p n -> p (a n)")).then_inc(weights_loaded, 16)

        @block.gpsimd
        def _(pool):
            g = nc.gpsimd
            g.iota(iota_e[:], pattern=[[1, E]], base=0, channel_multiplier=0, allow_small_or_imprecise_dtypes=True).then_inc(const_ready, 1)
            g.memset(ones[:], 1.0).then_inc(const_ready, 1)
            pool.wait_ge(const_ready, 2)
            g.affine_select(out=ident[:], in_=ones[:], compare_op=ALU.is_equal, fill=0.0, base=0,
                            pattern=[[-1, P]], channel_multiplier=1).then_inc(const_ready, 1)
            g.iota(iota_s[:], pattern=[[1, 200]], base=0, channel_multiplier=0,
                   allow_small_or_imprecise_dtypes=True).then_inc(const_ready, 1)
            g.iota(tok1[:], pattern=[[P, NT]], base=1, channel_multiplier=1,
                   allow_small_or_imprecise_dtypes=True).then_inc(const_ready, 1)
            g.iota(pe_id[:, 0:1], pattern=[[0, 1]], base=0, channel_multiplier=1,
                   allow_small_or_imprecise_dtypes=True).then_inc(const_ready, 1)
            g.affine_select(out=lower[:], in_=ones[0:E, 0:E], compare_op=ALU.is_gt, fill=0.0, base=0,
                            pattern=[[1, E]], channel_multiplier=-1).then_inc(const_ready, 1)
            g.affine_select(out=tri[:], in_=ones[:, 0:TOP * TOP].rearrange("p (a b) -> p a b", a=TOP),
                            compare_op=ALU.is_gt, fill=0.0, base=0,
                            pattern=[[1, TOP], [-1, TOP]], channel_multiplier=0).then_inc(const_ready, 1)
            g.affine_select(out=csel[:], in_=ones[0:E, 0:2], compare_op=ALU.is_ge, fill=0.0, base=E - 1,
                            pattern=[[-1, 2]], channel_multiplier=-1).then_inc(const_ready, 1)

            def gather(s, par):
                g.indirect_dma_start(out=xg[par], out_offset=None, in_=table,
                                     in_offset=bass.IndirectOffsetOnAxis(ap=idx[:, s:s + 1], axis=0),
                                     bounds_check=bound, oob_is_err=False).then_inc(gathered[par], 16)

            g.memset(neg_half[:], -0.5).then_inc(half_ready, 1)
            pool.wait_ge(half_ready, 1)
            for n in range(2 * NT):
                pool.wait_ge(mv_done, n + 1)
                if n:
                    pool.wait_ge(xn_ready if n % 2 == 0 else xq_ready, (n + 1) // 2)
                g.tensor_scalar(var_eps[:], mv[:, 1:2], EPS, None, ALU.add).then_inc(var_done, 1)
                pool.wait_ge(var_done, n + 1)
                g.tensor_tensor(rstd[:], var_eps[:], neg_half[:], ALU.pow).then_inc(rstd_done, 1)

            pool.wait_ge(c12_saved, NT)
            g.iota(iota_hi, pattern=[[1, STEPS], [0, TOP]], base=0, channel_multiplier=0,
                   allow_small_or_imprecise_dtypes=True).then_inc(S["iota_ready"], 1)
            g.iota(iota_lo, pattern=[[1, P], [0, TOP]], base=0, channel_multiplier=0,
                   allow_small_or_imprecise_dtypes=True).then_inc(S["iota_ready"], 1)
            bound = pool.to_reg(T - 1)
            pool.wait_ge(S["idx_ready"], 1)
            pool.wait_ge(S["wf_stored"], 16 * NT)
            pool.wait_ge(xn_stored, 16 * NT)
            pool.wait_ge(x1_stored, 16 * NT)
            gather(0, 0)
            gather(1, 1)
            pool.wait_ge(w_kept, 1)
            gather(2, 0)

            def step_of(i, par, peeled, last=False):
                s = 2 * i + par
                if not last:
                    wait_alone(pool, w_kept, s + 2)
                    g.tensor_copy(idx_now[:, 1 - par:2 - par], idx[:, ds(s + 3, 1)]).then_inc(idx_copied, 1)
                    wait_alone(pool, idx_copied, 4 * i + 2 * par + 1)
                    g.indirect_dma_start(out=xg[1 - par], out_offset=None, in_=table,
                                         in_offset=bass.IndirectOffsetOnAxis(ap=idx_now[:, 1 - par:2 - par], axis=0),
                                         bounds_check=bound, oob_is_err=False).then_inc(gathered[1 - par], 16)
                if not peeled:
                    wait_alone(pool, scattered[par], 16 * i)
                g.tensor_copy(idx_now[:, 2 + par:3 + par], idx[:, ds(s, 1)]).then_inc(idx_copied, 1)
                if peeled and par:
                    pool.wait_ge(scattered[0], 16)
                if not peeled:
                    first = pool.value_load(plan[0:1, ds(200 + s, 1)], min_val=0, max_val=1)
                    with pool.If(first > 0):
                        wait_alone(pool, scattered[0], 16 * i + 16 * par)
                        wait_alone(pool, scattered[1], 16 * i)
                wait_alone(pool, idx_copied, 4 * i + (par + 1 if last else 2 * par + 2))
                wait_alone(pool, y_ready, s + 1)
                g.indirect_dma_start(out=out, out_offset=bass.IndirectOffsetOnAxis(ap=idx_now[:, 2 + par:3 + par], axis=0),
                                     in_=y_sb[par], in_offset=None, bounds_check=bound, oob_is_err=False,
                                     compute_op=ALU.add).then_inc(scattered[par], 16)

            pool.wait_ge(S["plan_saved"], 3)
            step_of(0, 0, True)
            step_of(0, 1, True)
            more = pool.value_load(plan[0:1, more_at:more_at + 1], min_val=E // 2 - 1, max_val=STEPS // 2 - 1)
            with pool.Fori(1, more) as i:
                for par in range(2):
                    step_of(i, par, False)
            step_of(more, 0, False, last=True)
            step_of(more, 1, False, last=True)
            pool.wait_ge(scattered[0], 16 * more + 16)
            pool.wait_ge(scattered[1], 16 * more + 16)
            pool.wait_ge(gathered[0], 16 * more + 32)
            pool.wait_ge(gathered[1], 16 * more + 16)

        @block.scalar
        def _(act):
            a = nc.scalar

            def split_batch(b, first):
                act.wait_ge(k_loaded, 16 * (b + 1))
                if not first:
                    act.wait_ge(scores_done, TB * b)
                a.copy(K_HI, k_raw).then_inc(k_hi, 1)
                act.wait_ge(v_loaded, 16 * (b + 1))
                if not first:
                    act.wait_ge(readout_done, TB * b)
                a.copy(V_HI, v_raw).then_inc(v_hi, 1)

            def front(t, first):
                act.wait_ge(q_transposed, t + 1)
                if not first:
                    act.wait_ge(scores_done, t)
                a.copy(qT_hi[:].rearrange("p c n -> p (c n)"), b_q[:]).then_inc(qT_hi_ready, 1)

            def softmax(t, first):
                act.wait_ge(neg_max_done, t + 1)
                if not first:
                    act.wait_ge(p_transposed, t)
                a.activation(probs[:], scores[:], ACT.Exp, bias=neg_max[:, 0:1], accum_out=row_sum[:, 0:1]).then_inc(probs_ready, 1)

            def back(t, first):
                act.wait_ge(p_transposed, t + 1)
                if not first:
                    act.wait_ge(readout_done, t)
                a.copy(pT_hi[:].rearrange("p c n -> p (c n)"), b_p[:]).then_inc(pT_hi_ready, 1)

            def router(t, first):
                act.wait_ge(xn_transposed, t + 1)
                if not first:
                    act.wait_ge(logits_done, t)
                a.copy(xnT[:].rearrange("p c n -> p (c n)"), b_r[:]).then_inc(xnT_ready, 1)
                act.wait_ge(r_neg_done, t + 1)
                a.activation(r_exp[:], b_l[:, 0:E], ACT.Exp, bias=r_neg[:, 0:1], accum_out=r_sum[:, 0:1]).then_inc(r_exp_done, 1)
                act.wait_ge(probs_ready, 1)
                act.wait_ge(route_transposed, 2 * t + 2)
                a.copy(w12T[:, ds(t * P, P)], b_l[:, 256:384]).then_inc(w12_saved, 1)

            split_batch(0, True)
            for t in range(NT):
                if t % TB == 0 and t:
                    split_batch(t // TB, False)
                front(t, t == 0)
                softmax(t, t == 0)
                back(t, t == 0)
                router(t, t == 0)

            for t in range(NT):
                act.wait_ge(S["look_done"], t + 1)
                if t >= 2:
                    act.wait_ge(S["wf_stored"], 16 * (t - 1))
                a.copy(wf_sb[:, t % 2, :], (b_v, b_r)[t % 2][:, P:P + E]).then_inc(S["wf_saved"], 1)

            def xT(s, par):
                act.wait_ge(x_transposed, s + 1)
                a.copy(xT_hi[par].rearrange("p c n -> p (c n)"), b_q[:]).then_inc(xT_hi_ready, 1)

            def silu(s):
                act.wait_ge(gate_up_done, s + 1)
                a.activation(act_g, b_r[:, 0:F], ACT.Silu).then_inc(silu_done, 1)

            def hT(s):
                act.wait_ge(h_transposed, s + 1)
                a.copy(hT_hi[0:FP].rearrange("p c n -> p (c n)"), b_v[0:FP, 0:FC * P]).then_inc(hT_hi_ready, 1)

            def y(s, par, need):
                act.wait_ge(down_done, s + 3)
                if need is not None:
                    act.wait_ge(scattered[par], need)
                a.copy(y_sb[par], b_s[:, 0:D]).then_inc(y_ready, 1)

            def step_of(s, i, par, need):
                split_it = act.value_load(plan[1:2, ds(200 + s, 1)], min_val=0, max_val=1)

                def tile(piece):
                    hT(s - 1 if isinstance(s, int) else 2 * i + par)
                    xT(s + 1, par)
                    piece(0)
                    silu(s)
                    piece(1)
                    y(s - 1 if isinstance(s, int) else 2 * i + par, par, need)
                    piece(2)

                with act.If(split_it > 0):
                    e = act.value_load(plan[0:1, ds(s, 1)], min_val=0, max_val=E - 2)
                    hi, src = pieces((e + 1) % 3, 0), raw_pieces((e + 1) % 2)

                    def piece(j):
                        if j == 0:
                            wait_alone(act, down_done, s + 1)
                            wait_alone(act, weights_loaded, 32 * e + 64)
                        a.copy(hi[j], src[j]).then_inc(weights_hi, 1)
                    tile(piece)
                with act.Else():
                    tile(lambda j: None)

            act.wait_ge(weights_loaded, 32)
            for j in range(3):
                a.copy(pieces(0, 0)[j], raw_pieces(0)[j]).then_inc(weights_hi, 1)
            xT(0, 0)
            act.wait_ge(S["plan_saved"], 3)
            act.wait_ge(weights_loaded, 64)
            xT(1, 1)
            for j in range(3):
                a.copy(pieces(1, 0)[j], raw_pieces(1)[j]).then_inc(weights_hi, 1)
            silu(0)
            step_of(1, 0, 0, None)
            step_of(2, 0, 1, None)
            more = act.value_load(plan[0:1, more_at:more_at + 1], min_val=E // 2 - 1, max_val=STEPS // 2 - 1)
            with act.Fori(1, more) as i:
                for par in range(2):
                    step_of(2 * i + par + 1, i, par, 16 * i)
            hT(2 * more)
            silu(2 * more + 1)
            y(2 * more, 0, 16 * more)
            hT(2 * more + 1)
            y(2 * more + 1, 1, 16 * more)

        @block.tensor
        def _(pe):
            m = nc.tensor

            def split_product(o, left, right, n):
                last = None
                for j in range(n):
                    for k, (l, r) in enumerate(((0, 0), (0, 1), (1, 0))):
                        last = m.matmul(o, left[l](j), right[r](j), start=(j == 0 and k == 0), stop=(j == n - 1 and k == 2))
                return last

            def transposes(o, src, n):
                for j in range(n):
                    last = m.transpose(o[:, j * P:(j + 1) * P], src[:, j * P:(j + 1) * P], ident[:])
                return last

            def front(t, b, first):
                pe.wait_ge(xq_ready, t + 1)
                if not first:
                    pe.wait_ge(qT_lo_ready, t)
                transposes(b_q, xq, C).then_inc(q_transposed, 1)
                pe.wait_ge(k_lo, b + 1)
                pe.wait_ge(qT_lo_ready, t + 1)
                if not first:
                    pe.wait_ge(biased, t)
                for n in range(M // 512):
                    last = split_product(b_s[:, n * 512:(n + 1) * 512],
                                         (lambda j: qT_hi[:, j, :], lambda j: qT_lo[:, j, :]),
                                         (lambda j: kh[:, j, n * 512:(n + 1) * 512], lambda j: kl[:, j, n * 512:(n + 1) * 512]), C)
                last.then_inc(scores_done, 1)

            def back(t, b, first):
                pe.wait_ge(probs_ready, t + 1)
                if not first:
                    pe.wait_ge(pT_lo_ready, t)
                transposes(b_p, probs, MT).then_inc(p_transposed, 1)
                pe.wait_ge(v_lo, b + 1)
                pe.wait_ge(pT_lo_ready, t + 1)
                if not first:
                    pe.wait_ge(x1_ready, t)
                split_product(b_v[:, 0:D], (lambda j: pT_hi[:, j, :], lambda j: pT_lo[:, j, :]),
                              (lambda j: vh[:, j, :], lambda j: vl[:, j, :]), MT).then_inc(readout_done, 1)

            def router(t, first):
                pe.wait_ge(xn_ready, t + 1)
                if not first:
                    pe.wait_ge(xnT_ready, t)
                transposes(b_r, xn, C).then_inc(xn_transposed, 1)
                pe.wait_ge(small_loaded, 32)
                pe.wait_ge(xnT_ready, t + 1)
                if not first:
                    pe.wait_ge(w12_saved, t)
                    pe.wait_ge(c12_saved, t)
                for j in range(C):
                    last = m.matmul(b_l[:, 0:E], xnT[:, j, :], gate_w[:, j, :], start=(j == 0), stop=(j == C - 1))
                last.then_inc(logits_done, 1)
                pe.wait_ge(chosen_ready, t + 1)
                pe.wait_ge(r_exp_done, t + 1)
                ch = chosen[:, t].rearrange("p k h e -> p k (h e)")
                for k in range(SEL):
                    last = m.matmul(b_l[:, P:2 * P], ch[:, k, :], ident16[:], start=(k == 0), stop=(k == SEL - 1))
                last.then_inc(route_transposed, 1)
                pe.wait_ge(w12_ready, t + 1)
                pe.wait_ge(c12_saved, t + 1)
                m.transpose(b_l[:, 256:384], w12[:].rearrange("p h e -> p (h e)"), ident[:]).then_inc(route_transposed, 1)

            pe.wait_ge(const_ready, CONSTS)
            pe.wait_ge(ident_f16, 1)
            for t in range(NT):
                front(t, t // TB, t == 0)
                back(t, t // TB, t == 0)
                router(t, t == 0)

            pe.wait_ge(w12_saved, NT)
            pe.wait_ge(S["prim_done"], 1)
            m.matmul(b_q[:, 0:E], p64[0:E, :], ident[0:E, 0:E], start=True, stop=True)
            m.matmul(b_q[:, E:E + 1], dup[0:E, :], pcol[0:E, :], start=True, stop=True).then_inc(S["bsel_done"], 1)
            pe.wait_ge(S["map_done"], 2)
            m.transpose(b_r[0:E, 0:P], ir[:], ident[:]).then_inc(S["irT_done"], 1)
            for n in range(T // 512):
                o = (b_s, b_p)[n // 2][0:E, (n % 2) * 512:(n % 2 + 1) * 512]
                m.matmul(o, ir16[:], c12T[:, n * 512:(n + 1) * 512], start=True, stop=True).then_inc(S["cf_done"], 1)
            pe.wait_ge(S["total_done"], 1)
            m.matmul(b_q[0:E, 128:129], lower[:], stepsE[:, 0:1], start=True, stop=True)
            m.matmul(b_q[0:1, 132:133], stepsE[:, 0:1], ones[0:E, 0:1], start=True, stop=True).then_inc(S["bases_done"], 1)
            pe.wait_ge(S["plan_done"], 1)
            m.matmul(b_l[0:2, 0:400], csel[:], cmp[:].rearrange("e a s -> e (a s)"), start=True, stop=True).then_inc(S["bsel2_done"], 1)
            pe.wait_ge(S["irT_saved"], 1)
            pe.wait_ge(S["slots_done"], 1)
            for t in range(NT):
                o = (b_v, b_r)[t % 2]
                if t >= 2:
                    pe.wait_ge(S["look_done"], t - 1)
                    pe.wait_ge(S["wf_saved"], t - 1)
                m.matmul(o[:, 0:P], uniq[:, t * P:(t + 1) * P], irT[:], start=True, stop=True)
                m.matmul(o[:, P:P + E], w12T[:, t * P:(t + 1) * P], ir[:], start=True, stop=True).then_inc(S["ff_done"], 1)
            pe.wait_ge(S["plan_saved"], 3)
            for t in range(NT):
                pe.wait_ge(S["lo_ready"], t + 1)
                for k in range(TOP):
                    last = m.matmul(b_l[:, 0:STEPS], oh_lo[:, :, k], oh_hi[:, :, k],
                                    start=(t == 0 and k == 0), stop=(t == NT - 1 and k == TOP - 1))
                last.then_inc(S["list_done"], 1)

            def x_transpose(s, par, nth):
                pe.wait_ge(xT_lo_ready, s) if nth else None
                pe.wait_ge(gathered[par], nth)
                transposes(b_q, xg[par], C).then_inc(x_transposed, 1)

            def gate_up(s, par):
                e = pe.value_load(plan[0:1, ds(s, 1)], min_val=0, max_val=E - 1)
                pe.wait_ge(weights_lo, 3 * e + 3)
                pe.wait_ge(xT_lo_ready, s + 1)
                base = (e % 3) * (2 * WE)
                split_product(b_r[:, 0:F2], (lambda j: xT_hi[par][:, j, :], lambda j: xT_lo[par][:, j, :]),
                              (lambda j: split[:, ds(base + j * F2, F2)], lambda j: split[:, ds(base + WE + j * F2, F2)]), C).then_inc(gate_up_done, 1)

            def h_transpose(s):
                pe.wait_ge(hid_ready, s + 1)
                for j in range(FC):
                    last = m.transpose(b_v[0:FP, j * P:(j + 1) * P], hid[:, j * FP:(j + 1) * FP], ident[:])
                last.then_inc(h_transposed, 1)

            def down(s):
                e = pe.value_load(plan[0:1, ds(s, 1)], min_val=0, max_val=E - 1)
                base = (e % 3) * (2 * WE) + WI
                pe.wait_ge(hT_lo_ready, s + 1)
                pe.wait_ge(y_ready, s)
                split_product(b_s[:, 0:D], (lambda j: hT_hi[0:FP, j, :], lambda j: hT_lo[0:FP, j, :]),
                              (lambda j: split[0:FP, ds(base + j * D, D)], lambda j: split[0:FP, ds(base + WE + j * D, D)]), FC).then_inc(down_done, 1)

            pe.sem_inc(down_done, 2)
            pe.wait_ge(S["idx_ready"], 1)
            pe.wait_ge(gathered[0], 16)
            transposes(b_q, xg[0], C).then_inc(x_transposed, 1)
            pe.wait_ge(gathered[1], 16)
            pe.wait_ge(xT_lo_ready, 1)
            transposes(b_q, xg[1], C).then_inc(x_transposed, 1)
            gate_up(0, 0)
            more = pe.value_load(plan[0:1, more_at:more_at + 1], min_val=E // 2 - 1, max_val=STEPS // 2 - 1)
            h_transpose(0)
            with pe.Fori(0, more) as i:
                for par in range(2):
                    s = 2 * i + par + 1
                    pe.wait_ge(gathered[par], 16 * i + 32)
                    pe.wait_ge(xT_lo_ready, 2 * i + par + 2)
                    transposes(b_q, xg[par], C).then_inc(x_transposed, 1)
                    gate_up(s, 1 - par)
                    down(2 * i + par)
                    h_transpose(s)
            gate_up(2 * more + 1, 1)
            down(2 * more)
            h_transpose(2 * more + 1)
            down(2 * more + 1)

        @block.vector
        def _(dve):
            v = nc.vector

            def layer_norm(src, dst, n, first, ready, dst_free):
                v.bn_stats(stats[:], src).then_inc(stats_done, 1)
                dve.wait_ge(stats_done, n + 1)
                v.bn_aggr(mv[:], stats[:]).then_inc(mv_done, 1)
                dve.wait_ge(mv_done, n + 1)
                for s_, n_ in dst_free:
                    dve.wait_ge(s_, n_)
                dve.wait_ge(rstd_done, n + 1)
                v.tensor_scalar(dst, src, mv[:, 0:1], rstd[:, 0:1], ALU.subtract, ALU.mult).then_inc(ready, 1)

            def split_batch(b, first):
                dve.wait_ge(k_hi, b + 1)
                v.tensor_tensor(K_LO, k_raw, K_HI, ALU.subtract).then_inc(k_lo, 1)
                dve.wait_ge(v_hi, b + 1)
                v.tensor_tensor(V_LO, v_raw, V_HI, ALU.subtract).then_inc(v_lo, 1)
                if first:
                    dve.wait_ge(small_loaded, 32)
                else:
                    dve.wait_ge(biased, TB * b)
                v.tensor_scalar(mask_bias[:], mask_u8[:, ds(b * M, M)], BIG, -BIG, ALU.mult, ALU.add).then_inc(bias_ready, 1)

            def front(t, b, first):
                dve.wait_ge(x_loaded, 16 * (t + 1))
                layer_norm(x_all[:, t, :], xq[:], 2 * t, first, xq_ready, [] if first else [(q_transposed, t)])
                dve.wait_ge(qT_hi_ready, t + 1)
                v.tensor_tensor(qT_lo[:].rearrange("p c n -> p (c n)"), b_q[:], qT_hi[:].rearrange("p c n -> p (c n)"), ALU.subtract).then_inc(qT_lo_ready, 1)
                dve.wait_ge(scores_done, t + 1)
                dve.wait_ge(bias_ready, b + 1)
                if not first:
                    dve.wait_ge(probs_ready, t)
                v.scalar_tensor_tensor(out=scores[:], in0=b_s[:], scalar=SCALE, in1=mask_bias[:], op0=ALU.mult, op1=ALU.add).then_inc(biased, 1)
                dve.wait_ge(biased, t + 1)
                v.tensor_reduce(neg_max[:], scores[:], AX.X, ALU.max, negate=True).then_inc(neg_max_done, 1)

            def back(t, b, first):
                dve.wait_ge(probs_ready, t + 1)
                v.reciprocal(row_inv[:, 0:1], row_sum[:]).then_inc(inv_done, 1)
                dve.wait_ge(inv_done, t + 1)
                v.tensor_tensor(row_inv[:, 1:2], row_inv[:, 0:1], valid[:, ds(b, 1)], ALU.mult).then_inc(inv_valid, 1)
                dve.wait_ge(pT_hi_ready, t + 1)
                v.tensor_tensor(pT_lo[:].rearrange("p c n -> p (c n)"), b_p[:], pT_hi[:].rearrange("p c n -> p (c n)"), ALU.subtract).then_inc(pT_lo_ready, 1)
                dve.wait_ge(inv_valid, t + 1)
                dve.wait_ge(readout_done, t + 1)
                xs = x_all[:, t, :]
                v.scalar_tensor_tensor(out=xs, in0=b_v[:, 0:D], scalar=row_inv[:, 1:2], in1=xs, op0=ALU.mult, op1=ALU.add).then_inc(x1_ready, 1)
                dve.wait_ge(x1_ready, t + 1)
                layer_norm(xs, xn[:], 2 * t + 1, first, xn_ready, [] if first else [(xn_stored, 16 * t), (xn_transposed, t)])

            def router(t, first):
                dve.wait_ge(logits_done, t + 1)
                v.tensor_reduce(r_neg[:], b_l[:, 0:E], AX.X, ALU.max, negate=True).then_inc(r_neg_done, 1)
                dve.wait_ge(r_exp_done, t + 1)
                base = 8 * t
                v.reciprocal(r_sum[:, 1:2], r_sum[:, 0:1]).then_inc(r_step, 1)
                dve.wait_ge(r_step, base + 1)
                v.tensor_scalar(r_probs[:], r_exp[:], r_sum[:, 1:2], None, ALU.mult).then_inc(r_step, 1)
                dve.wait_ge(r_step, base + 2)
                v.max(top_val[:], r_probs[:]).then_inc(r_step, 1)
                dve.wait_ge(r_step, base + 3)
                v.max_index(top_idx[:], top_val[:], r_probs[:]).then_inc(r_step, 1)
                v.tensor_reduce(r_sum[:, 2:3], top_val[:], AX.X, ALU.add).then_inc(r_step, 1)
                dve.wait_ge(r_step, base + 5)
                v.tensor_copy(top_e[:], top_idx[:]).then_inc(r_step, 1)
                v.reciprocal(r_sum[:, 3:4], r_sum[:, 2:3]).then_inc(r_step, 1)
                dve.wait_ge(r_step, base + 7)
                v.tensor_scalar(top_w[:], top_val[:], r_sum[:, 3:4], None, ALU.mult).then_inc(r_step, 1)
                v.tensor_tensor(chosen[:, t], iota_e[:].unsqueeze(1).unsqueeze(1).broadcast_to([P, SEL, 2, E]),
                                top_e[:].rearrange("p (h k) -> p k h", h=2).unsqueeze(3).broadcast_to([P, SEL, 2, E]), ALU.is_equal).then_inc(chosen_ready, 1)
                dve.wait_ge(r_step, base + 8)
                dve.wait_ge(chosen_ready, t + 1)
                v.tensor_tensor(weighed[:], chosen[:, t], top_w[:].rearrange("p (h k) -> p k h", h=2).unsqueeze(3).broadcast_to([P, SEL, 2, E]), ALU.mult).then_inc(w_step, 1)
                dve.wait_ge(w_step, t + 1)
                if not first:
                    dve.wait_ge(route_transposed, 2 * t)
                v.tensor_reduce(w12[:], weighed[:].rearrange("p k h e -> p h e k"), AX.X, ALU.add).then_inc(w12_ready, 1)
                dve.wait_ge(route_transposed, 2 * t + 1)
                v.tensor_copy(c12T[:, ds(t * P, P)], b_l[:, P:2 * P]).then_inc(c12_saved, 1)

            dve.wait_ge(const_ready, CONSTS)
            v.tensor_copy(ident16[:], ident[:]).then_inc(ident_f16, 1)
            dve.wait_ge(small_loaded, 32)
            v.tensor_reduce(valid[:], mask_u8[:].rearrange("p (b m) -> p b m", b=B), AX.X, ALU.max).then_inc(valid_ready, 1)
            split_batch(0, True)
            for t in range(NT):
                if t % TB == 0 and t:
                    split_batch(t // TB, False)
                front(t, t // TB, t == 0)
                back(t, t // TB, t == 0)
                router(t, t == 0)

            step = chain(dve, "map_step")
            step(v.tensor_scalar(pe_id[:, 1:2], pe_id[:, 0:1], float(E), None, ALU.is_ge))
            step(v.scalar_tensor_tensor(out=pe_id[:, 2:3], in0=pe_id[:, 1:2], scalar=-float(E), in1=pe_id[:, 0:1], op0=ALU.mult, op1=ALU.add))
            step(v.tensor_copy(dup[0:E, 0:E], ident[0:E, 0:E]))
            step(v.tensor_copy(dup[0:E, E:P], ident[0:E, 0:E]))
            step(v.memset(ones_w, 1.0))
            dve.wait_ge(c12_saved, NT)
            step(v.tensor_reduce(reroute[:, 3:4], c12T[:], AX.X, ALU.max))
            step(v.tensor_scalar(pcol[:], reroute[:, 3:4], 0.0, None, ALU.is_gt))
            v.tensor_scalar(p64[0:E, :], ones[0:E, :], pcol[0:E, 0:1], None, ALU.mult).then_inc(S["prim_done"], 1)
            dve.wait_ge(S["sim_loaded"], 32)
            step(v.tensor_scalar(cand[:], iota_e[:], pe_id[:, 2:3], None, ALU.is_equal))
            step(v.tensor_scalar(ir[:], cand[:], -1.0, 1.0, ALU.mult, ALU.add))
            step(v.tensor_tensor(simd[:], simd[:], ir[:], ALU.mult))
            step(v.tensor_tensor(simd[:], simd[:], cand[:], ALU.add))
            dve.wait_ge(S["bsel_done"], 1)
            step(v.tensor_scalar(cand[:], b_q[:, 0:E], -1.0, 3.0e38, ALU.add, ALU.mult))
            step(v.tensor_tensor(cand[:], cand[:], simd[:], ALU.add))
            step(v.max(best_v[:], cand[:]))
            step(v.max_index(best_i[:], best_v[:], cand[:]))
            step(v.tensor_scalar(reroute[:, 0:1], best_v[:, 0:1], THRESH, None, ALU.is_ge))
            step(v.tensor_tensor(reroute[:, 0:1], reroute[:, 0:1], pcol[:], ALU.mult))
            step(v.tensor_scalar(reroute[:, 1:2], b_q[:, E:E + 1], -1.0, 1.0, ALU.mult, ALU.add))
            step(v.tensor_tensor(reroute[:, 0:1], reroute[:, 0:1], reroute[:, 1:2], ALU.mult))
            step(v.tensor_tensor(reroute[:, 0:1], reroute[:, 0:1], pe_id[:, 1:2], ALU.mult))
            step(v.tensor_copy(reroute[:, 2:3], best_i[:, 0:1]))
            step(v.tensor_tensor(reroute[:, 2:3], reroute[:, 2:3], pe_id[:, 2:3], ALU.subtract))
            step(v.scalar_tensor_tensor(out=reroute[:, 3:4], in0=reroute[:, 2:3], scalar=reroute[:, 0:1], in1=pe_id[:, 2:3], op0=ALU.mult, op1=ALU.add))
            v.tensor_scalar(ir[:], iota_e[:], reroute[:, 3:4], None, ALU.is_equal).then_inc(S["map_done"], 1)
            v.tensor_scalar(ir16[:], iota_e[:], reroute[:, 3:4], None, ALU.is_equal).then_inc(S["map_done"], 1)
            dve.wait_ge(S["irT_done"], 1)
            v.tensor_copy(irT[:], b_r[0:E, 0:P]).then_inc(S["irT_saved"], 1)
            for n in range(T // 512):
                dve.wait_ge(S["cf_done"], n + 1)
                c = slice(n * 512, (n + 1) * 512)
                v.tensor_scalar(uniq[:, c], (b_s, b_p)[n // 2][0:E, (n % 2) * 512:(n % 2 + 1) * 512], 1.0, None, ALU.min).then_inc(S["uniq_done"], 1)
                dve.wait_ge(S["uniq_done"], n + 1)
                if n:
                    dve.wait_ge(S["scan_done"], n)
                v.tensor_tensor_scan(out=scan[:, c], data0=ones_w[:, c], data1=uniq[:, c],
                                     initial=0.0 if n == 0 else scan[:, n * 512 - 1:n * 512], op0=ALU.mult, op1=ALU.add).then_inc(S["scan_done"], 1)
            dve.wait_ge(S["scan_done"], T // 512)
            step(v.tensor_scalar(stepsE[:, 1:2], scan[:, T - 1:T], 1.0 / P, 0.5 - 0.5 / P, ALU.mult, ALU.add))
            step(v.tensor_scalar(stepsE[:, 2:3], stepsE[:, 1:2], ROUND, -ROUND, ALU.add, ALU.add))
            v.tensor_scalar(stepsE[:, 0:1], stepsE[:, 2:3], 1.0, None, ALU.max).then_inc(S["total_done"], 1)
            dve.wait_ge(S["bases_done"], 1)
            step(v.tensor_copy(stepsE[:, 3:4], b_q[0:E, 128:129]))
            step(v.tensor_scalar(stepsE[:, 1:2], stepsE[:, 3:4], float(P), None, ALU.mult))
            step(v.tensor_scalar(cmp[:, 0, :], iota_s[:], stepsE[:, 3:4], None, ALU.is_ge))
            v.tensor_scalar(cmp[:, 1, :], iota_s[:], stepsE[:, 3:4], None, ALU.is_equal).then_inc(S["plan_done"], 1)
            v.scalar_tensor_tensor(out=uniq, in0=scan, scalar=stepsE[:, 1:2], in1=uniq, op0=ALU.add, op1=ALU.subtract).then_inc(S["slots_done"], 1)
            dve.wait_ge(S["bsel2_done"], 1)
            v.tensor_scalar(plan[0:1, 0:200], b_l[0:1, 0:200], -1.0, None, ALU.add).then_inc(S["plan_saved"], 1)
            v.tensor_copy(plan[:, 200:400], b_l[0:2, 200:400]).then_inc(S["plan_saved"], 1)
            step(v.tensor_scalar(reroute[0:1, 0:1], b_q[0:1, 132:133], 0.5, 0.25, ALU.mult, ALU.add))
            step(v.tensor_scalar(reroute[0:1, 1:2], reroute[0:1, 0:1], ROUND, -ROUND, ALU.add, ALU.add))
            v.tensor_scalar(plan[0:1, more_at:more_at + 1], reroute[0:1, 1:2], -1.0, None, ALU.add).then_inc(S["plan_saved"], 1)
            for t in range(NT):
                dve.wait_ge(S["ff_done"], t + 1)
                ff = (b_v, b_r)[t % 2][:, 0:P].unsqueeze(1).broadcast_to([P, SEL, P])
                v.tensor_tensor(lookm[:].rearrange("p k h e -> p k (h e)"), chosen[:, t].rearrange("p k h e -> p k (h e)"), ff, ALU.mult).then_inc(S["look_done"], 1)
                dve.wait_ge(S["look_done"], t + 1)
                v.tensor_reduce(slots[:, t * TOP:(t + 1) * TOP], lookm[:].rearrange("p k h e -> p (k h) e"), AX.X, ALU.add).then_inc(S["g_ready"], 1)
                dve.wait_ge(S["g_ready"], t + 1)
            s3 = slots[:].rearrange("p (t k) -> p t k", k=TOP)
            step(v.tensor_tensor(eqk, s3.unsqueeze(3).broadcast_to([P, NT, TOP, TOP]), s3.unsqueeze(2).broadcast_to([P, NT, TOP, TOP]), ALU.is_equal))
            step(v.tensor_tensor(eqk, eqk, tri[:].unsqueeze(1).broadcast_to([P, NT, TOP, TOP]), ALU.mult))
            step(v.tensor_reduce(seen[:], eqk.rearrange("p t k j -> p (t k) j"), AX.X, ALU.max))
            step(v.tensor_scalar(lo32[:], slots[:], 1.0 / P, -0.5 + 0.5 / P, ALU.mult, ALU.add))
            step(v.tensor_scalar(hi32[:], lo32[:], ROUND, -ROUND, ALU.add, ALU.add))
            step(v.tensor_copy(hi16[:], hi32[:]))
            step(v.scalar_tensor_tensor(out=lo32[:], in0=hi32[:], scalar=-float(P), in1=slots[:], op0=ALU.mult, op1=ALU.add))
            step(v.scalar_tensor_tensor(out=lo16[:], in0=seen[:], scalar=-2.0 * P, in1=lo32[:], op0=ALU.mult, op1=ALU.add))
            dve.wait_ge(S["iota_ready"], 2)
            for t in range(NT):
                k8 = slice(t * TOP, (t + 1) * TOP)
                if t:
                    dve.wait_ge(S["list_done"], t)
                v.tensor_tensor(oh_hi, iota_hi, hi16[:, k8].unsqueeze(1).broadcast_to([P, STEPS, TOP]), ALU.is_equal).then_inc(S["hi_ready"], 1)
                step(v.tensor_tensor(oh_lo, iota_lo, lo16[:, k8].unsqueeze(1).broadcast_to([P, P, TOP]), ALU.is_equal))
                dve.wait_ge(S["hi_ready"], t + 1)
                v.tensor_scalar(oh_lo, oh_lo, tok1[:, t:t + 1], None, ALU.mult).then_inc(S["lo_ready"], 1)
            step(v.memset(idxf[:], FAR))
            dve.wait_ge(S["list_done"], NT)
            step(v.tensor_scalar(idxf[:, 0:STEPS], b_l[:, 0:STEPS], 0.0, FAR, ALU.is_equal, ALU.mult))
            step(v.tensor_tensor(idxf[:, 0:STEPS], idxf[:, 0:STEPS], b_l[:, 0:STEPS], ALU.add))
            v.tensor_scalar(idx[:], idxf[:], -1.0, None, ALU.add).then_inc(S["idx_ready"], 1)

            def xT(s, par):
                dve.wait_ge(xT_hi_ready, s + 1)
                v.tensor_tensor(xT_lo[par].rearrange("p c n -> p (c n)"), b_q[:], xT_hi[par].rearrange("p c n -> p (c n)"), ALU.subtract).then_inc(xT_lo_ready, 1)
                v.tensor_copy(w_row[par], xg[par][:, D:ROW]).then_inc(w_kept, 1)

            def hidden(s, par):
                e = dve.value_load(plan[0:1, ds(s, 1)], min_val=0, max_val=E - 1)
                dve.wait_ge(w_kept, s + 1)
                dve.wait_ge(silu_done, s + 1)
                v.scalar_tensor_tensor(out=hid, in0=act_g, scalar=w_row[par][:, ds(e, 1)], in1=b_r[:, F:F2], op0=ALU.mult, op1=ALU.mult).then_inc(hid_ready, 1)

            def hT(s):
                dve.wait_ge(hT_hi_ready, s + 1)
                v.tensor_tensor(hT_lo[0:FP].rearrange("p c n -> p (c n)"), b_v[0:FP, 0:FC * P], hT_hi[0:FP].rearrange("p c n -> p (c n)"), ALU.subtract).then_inc(hT_lo_ready, 1)

            def step_of(s, i, par):
                split_it = dve.value_load(plan[1:2, ds(200 + s, 1)], min_val=0, max_val=1)

                def tile(piece):
                    hT(2 * i + par)
                    xT(s + 1, par)
                    piece(0)
                    hidden(s, 1 - par)
                    piece(1)
                    piece(2)

                with dve.If(split_it > 0):
                    e = dve.value_load(plan[0:1, ds(s, 1)], min_val=0, max_val=E - 2)
                    lo, hi, src = pieces((e + 1) % 3, 1), pieces((e + 1) % 3, 0), raw_pieces((e + 1) % 2)

                    def piece(j):
                        wait_alone(dve, weights_hi, 3 * e + 4 + j)
                        v.tensor_tensor(lo[j], src[j], hi[j], ALU.subtract).then_inc(weights_lo, 1)
                    tile(piece)
                with dve.Else():
                    tile(lambda j: None)

            for j in range(3):
                dve.wait_ge(weights_hi, j + 1)
                v.tensor_tensor(pieces(0, 1)[j], raw_pieces(0)[j], pieces(0, 0)[j], ALU.subtract).then_inc(weights_lo, 1)
            xT(0, 0)
            xT(1, 1)
            for j in range(3):
                dve.wait_ge(weights_hi, j + 4)
                v.tensor_tensor(pieces(1, 1)[j], raw_pieces(1)[j], pieces(1, 0)[j], ALU.subtract).then_inc(weights_lo, 1)
            hidden(0, 0)
            more = dve.value_load(plan[0:1, more_at:more_at + 1], min_val=E // 2 - 1, max_val=STEPS // 2 - 1)
            with dve.Fori(0, more) as i:
                for par in range(2):
                    step_of(2 * i + par + 1, i, par)
            hT(2 * more)
            hidden(2 * more + 1, 1)
            hT(2 * more + 1)


_INS = ["x", "ctx", "ctxT", "mask", "gateT", "w_in", "w_out", "sim"]


def kernel(x, ctx_2048, mask_BxS2_bk0, L0_ffn_gate_weight, L0_ffn_gate_up_proj, L0_ffn_down_proj, L0_ffn_similarity):
    import numpy as np
    import concourse.bacc as bacc
    from concourse.bass_utils import run_bass_kernel_spmd

    def con(a):
        return np.ascontiguousarray(a)

    x, ctx = np.asarray(x), np.asarray(ctx_2048)
    up, down = np.asarray(L0_ffn_gate_up_proj), np.asarray(L0_ffn_down_proj)
    E, F2, D = up.shape
    F = down.shape[2]
    arrays = {
        "x": con(x.reshape(-1, D)),
        "ctx": con(ctx),
        "ctxT": con(ctx.transpose(0, 2, 1)),
        "mask": con(np.asarray(mask_BxS2_bk0)),
        "gateT": con(np.asarray(L0_ffn_gate_weight).T),
        "w_in": con(up.reshape(E, F2, D // P, P).transpose(0, 3, 2, 1).reshape(E, P, -1)),
        "w_out": con(down.reshape(E, D, 2, F // 2).transpose(0, 3, 2, 1).reshape(E, F // 2, -1)),
        "sim": con(np.asarray(L0_ffn_similarity)),
    }
    nc = bacc.Bacc("TRN2", target_bir_lowering=False, num_devices=1)
    args = [nc.dram_tensor(n, arrays[n].shape, mybir.dt.from_np(arrays[n].dtype), kind="ExternalInput").ap() for n in _INS]
    out = nc.dram_tensor("out", list(arrays["x"].shape), F32, kind="ExternalOutput").ap()
    xattn_ffn(nc, *args, out)
    r = run_bass_kernel_spmd(nc, [arrays], core_ids=[0])
    return r.results[0]["out"].reshape(x.shape)
```
